# Optimizing a Trainium2 kernel written in Bass

```python
import numpy as np
import jax
import jax.numpy as jnp

def _softmax(x, axis=-1):
    return jax.nn.softmax(x, axis=axis)

def _gelu(x):
    return jax.nn.gelu(x, approximate=True)

def _silu(x):
    return jax.nn.silu(x)

def _sigmoid(x):
    return jax.nn.sigmoid(x)

def _layernorm(x, axis=-1, eps=1e-05):
    m = jnp.mean(x, axis=axis, keepdims=True)
    v = jnp.var(x, axis=axis, keepdims=True)
    return (x - m) / jnp.sqrt(v + eps)

def _scatter_add(tgt, idx, src, axis=0):
    return tgt.at[idx].add(src)

def _segment_sum(src, seg, n):
    return jax.ops.segment_sum(src, seg, n)
kernel_name = 'mk_decoder_postln_d1_seqx_r4_bfa84f'

def setup_inputs(seed: int=0):
    np.random.seed(seed)
    _w = jnp.asarray

    def _rec_inputs():
        import jax
        import jax.numpy as jnp
        _rk = jax.random.key(seed)
        x = -0.0002928 + 1 * jax.random.normal(jax.random.fold_in(_rk, 1), (8, 512, 256), jnp.float32)
        _lenS = 512 - jax.random.randint(jax.random.fold_in(_rk, 7), (8,), 0, max(1, 512 // 4) + 1, jnp.int32)
        _lenS2 = 512 - jax.random.randint(jax.random.fold_in(_rk, 8), (8,), 0, max(1, 512 // 4) + 1, jnp.int32)
        _ctx_1024P = jax.random.normal(jax.random.fold_in(_rk, 11), (8, 16, 256), jnp.float32)
        _ctx_1024c = jax.random.dirichlet(jax.random.fold_in(_rk, 511), 0.3 * jnp.ones((16,), jnp.float32), (8, 512))
        _ctx_1024t = jnp.einsum('bsk,bkd->bsd', _ctx_1024c, _ctx_1024P)
        _ctx_1024t = _ctx_1024t * jax.lax.rsqrt(jnp.mean(jnp.square(_ctx_1024t)) + 1e-12) * 0.953939
        ctx_1024 = -1.39393e-06 + 0.999914 * (_ctx_1024t + 0.3 * jax.random.normal(jax.random.fold_in(_rk, 611), (8, 512, 256), jnp.float32))
        return (x, ctx_1024)
    x, ctx_1024 = _rec_inputs()

    def _L0_attn_setup():
        import jax, jax.numpy as jnp
        import numpy as np
        DECAY = 0.99
        LR = 0.01

        def _reference_tuple_inner(x, Wk, bk, Wv, bv, Wq, bq, Wo, bo):
            B, S, D = x.shape
            M = Wk.shape[0]
            k = jnp.einsum('bsd,md->bsm', x, Wk) + bk
            v = jnp.einsum('bsd,md->bsm', x, Wv) + bv
            q = jnp.einsum('bsd,md->bsm', x, Wq) + bq

            def step(state, kvq):
                k_t, v_t, q_t = kvq
                out_t = jnp.einsum('bij,bj->bi', state, q_t)
                state = DECAY * state + LR * jnp.einsum('bi,bj->bij', v_t, k_t)
                return (state, out_t)
            state0 = jnp.zeros((B, M, M), x.dtype)
            xs = (jnp.swapaxes(k, 0, 1), jnp.swapaxes(v, 0, 1), jnp.swapaxes(q, 0, 1))
            state, outs = jax.lax.scan(step, state0, xs)
            outs = jnp.swapaxes(outs, 0, 1)
            y = jnp.einsum('bsm,dm->bsd', outs, Wo) + bo
            return (y, state)
        key = jax.random.key(seed)
        ks = jax.random.split(key, 6)
        B, S, D, M = (4, 1024, 256, 128)
        sD = 1.0 / np.sqrt(D)
        sM = 1.0 / np.sqrt(M)
        return {'x': jax.random.normal(ks[0], (B, S, D), dtype=jnp.float32), 'Wk': jax.random.uniform(ks[1], (M, D), jnp.float32, -sD, sD), 'bk': jnp.zeros((M,), jnp.float32), 'Wv': jax.random.uniform(ks[2], (M, D), jnp.float32, -sD, sD), 'bv': jnp.zeros((M,), jnp.float32), 'Wq': jax.random.uniform(ks[3], (M, D), jnp.float32, -sD, sD), 'bq': jnp.zeros((M,), jnp.float32), 'Wo': jax.random.uniform(ks[4], (D, M), jnp.float32, -sM, sM), 'bo': jnp.zeros((D,), jnp.float32)}
    _L0_attn_all = _L0_attn_setup()
    _L0_attn_in = {k: v for k, v in _L0_attn_all.items() if k in ('Wk', 'bk', 'Wv', 'bv', 'Wq', 'bq', 'Wo', 'bo')}
    del _L0_attn_all

    def _L0_xattn_setup():
        import jax, jax.numpy as jnp
        import numpy as np
        D_MODEL = 256
        N_HEADS = 16
        D_K = D_MODEL // N_HEADS
        key = jax.random.key(seed)
        ks = jax.random.split(key, 11)
        B, S = (2, 512)
        scale = 0.02
        inp = {'q': jax.random.normal(ks[0], (B, S, D_MODEL), jnp.float32), 'k': jax.random.normal(ks[1], (B, S, D_MODEL), jnp.float32), 'v': jax.random.normal(ks[2], (B, S, D_MODEL), jnp.float32), 'w_q': jax.random.normal(ks[3], (D_MODEL, D_MODEL), jnp.float32) * scale, 'b_q': jnp.zeros((D_MODEL,), jnp.float32), 'w_k': jax.random.normal(ks[4], (D_MODEL, D_MODEL), jnp.float32) * scale, 'b_k': jnp.zeros((D_MODEL,), jnp.float32), 'w_v': jax.random.normal(ks[5], (D_MODEL, D_MODEL), jnp.float32) * scale, 'b_v': jnp.zeros((D_MODEL,), jnp.float32), 'w_o': jax.random.normal(ks[6], (D_MODEL, D_MODEL), jnp.float32) * scale, 'b_o': jnp.zeros((D_MODEL,), jnp.float32)}
        return inp
    _L0_xattn_all = _L0_xattn_setup()
    _L0_xattn_in = {k: v for k, v in _L0_xattn_all.items() if k in ('w_q', 'b_q', 'w_k', 'b_k', 'w_v', 'b_v', 'w_o', 'b_o')}
    del _L0_xattn_all

    def _L0_ffn_setup():
        import jax, jax.numpy as jnp
        import numpy as np
        NUM_HEADS = 16
        TOP_K = 2
        key = jax.random.key(seed)
        ks = jax.random.split(key, 5)
        B, S, D, E = (4, 512, 256, 8)
        scale = 0.02
        return {'x': jax.random.normal(ks[0], (B, S, D), dtype=jnp.float32), 'W_qkv': jax.random.normal(ks[1], (D, 3 * D), dtype=jnp.float32) * scale, 'b_qkv': jnp.zeros((3 * D,), dtype=jnp.float32), 'W_gate': jax.random.normal(ks[2], (D, E), dtype=jnp.float32) * scale, 'b_gate': jnp.zeros((E,), dtype=jnp.float32), 'W_experts': jax.random.normal(ks[3], (E, D, D), dtype=jnp.float32) * scale, 'b_experts': jnp.zeros((E, D), dtype=jnp.float32)}
    _L0_ffn_all = _L0_ffn_setup()
    _L0_ffn_in = {k: v for k, v in _L0_ffn_all.items() if k in ('W_qkv', 'b_qkv', 'W_gate', 'b_gate', 'W_experts', 'b_experts')}
    del _L0_ffn_all
    return {'x': x, 'ctx_1024': ctx_1024, 'L0_attn_Wk': _L0_attn_in['Wk'], 'L0_attn_bk': _L0_attn_in['bk'], 'L0_attn_Wv': _L0_attn_in['Wv'], 'L0_attn_bv': _L0_attn_in['bv'], 'L0_attn_Wq': _L0_attn_in['Wq'], 'L0_attn_bq': _L0_attn_in['bq'], 'L0_attn_Wo': _L0_attn_in['Wo'], 'L0_attn_bo': _L0_attn_in['bo'], 'L0_xattn_w_q': _L0_xattn_in['w_q'], 'L0_xattn_b_q': _L0_xattn_in['b_q'], 'L0_xattn_w_k': _L0_xattn_in['w_k'], 'L0_xattn_b_k': _L0_xattn_in['b_k'], 'L0_xattn_w_v': _L0_xattn_in['w_v'], 'L0_xattn_b_v': _L0_xattn_in['b_v'], 'L0_xattn_w_o': _L0_xattn_in['w_o'], 'L0_xattn_b_o': _L0_xattn_in['b_o'], 'L0_ffn_W_qkv': _L0_ffn_in['W_qkv'], 'L0_ffn_b_qkv': _L0_ffn_in['b_qkv'], 'L0_ffn_W_gate': _L0_ffn_in['W_gate'], 'L0_ffn_b_gate': _L0_ffn_in['b_gate'], 'L0_ffn_W_experts': _L0_ffn_in['W_experts'], 'L0_ffn_b_experts': _L0_ffn_in['b_experts']}

def reference(x, ctx_1024, L0_attn_Wk, L0_attn_bk, L0_attn_Wv, L0_attn_bv, L0_attn_Wq, L0_attn_bq, L0_attn_Wo, L0_attn_bo, L0_xattn_w_q, L0_xattn_b_q, L0_xattn_w_k, L0_xattn_b_k, L0_xattn_w_v, L0_xattn_b_v, L0_xattn_w_o, L0_xattn_b_o, L0_ffn_W_qkv, L0_ffn_b_qkv, L0_ffn_W_gate, L0_ffn_b_gate, L0_ffn_W_experts, L0_ffn_b_experts):
    import jax
    import jax.numpy as jnp

    def _L0_attn_ref(x, Wk, bk, Wv, bv, Wq, bq, Wo, bo):
        import jax, jax.numpy as jnp
        import numpy as np
        DECAY = 0.99
        LR = 0.01

        def _reference_tuple_inner(x, Wk, bk, Wv, bv, Wq, bq, Wo, bo):
            B, S, D = x.shape
            M = Wk.shape[0]
            k = jnp.einsum('bsd,md->bsm', x, Wk) + bk
            v = jnp.einsum('bsd,md->bsm', x, Wv) + bv
            q = jnp.einsum('bsd,md->bsm', x, Wq) + bq

            def step(state, kvq):
                k_t, v_t, q_t = kvq
                out_t = jnp.einsum('bij,bj->bi', state, q_t)
                state = DECAY * state + LR * jnp.einsum('bi,bj->bij', v_t, k_t)
                return (state, out_t)
            state0 = jnp.zeros((B, M, M), x.dtype)
            xs = (jnp.swapaxes(k, 0, 1), jnp.swapaxes(v, 0, 1), jnp.swapaxes(q, 0, 1))
            state, outs = jax.lax.scan(step, state0, xs)
            outs = jnp.swapaxes(outs, 0, 1)
            y = jnp.einsum('bsm,dm->bsd', outs, Wo) + bo
            return (y, state)
        return _reference_tuple_inner(x, Wk, bk, Wv, bv, Wq, bq, Wo, bo)[0]

    def _L0_xattn_ref(q, k, v, w_q, b_q, w_k, b_k, w_v, b_v, w_o, b_o):
        import jax, jax.numpy as jnp
        import numpy as np
        D_MODEL = 256
        N_HEADS = 16
        D_K = D_MODEL // N_HEADS
        B, S, _ = q.shape

        def proj(x, w, b):
            return (x @ w.T + b).reshape(B, S, N_HEADS, D_K).transpose(0, 2, 1, 3)
        qh = proj(q, w_q, b_q)
        kh = proj(k, w_k, b_k)
        vh = proj(v, w_v, b_v)
        scores = jnp.einsum('bhqd,bhkd->bhqk', qh, kh) / jnp.sqrt(jnp.asarray(D_K, jnp.float32))
        attn = jax.nn.softmax(scores, axis=-1)
        out = jnp.einsum('bhqk,bhkd->bhqd', attn, vh)
        out = out.transpose(0, 2, 1, 3).reshape(B, S, D_MODEL)
        return out @ w_o.T + b_o

    def _L0_ffn_ref(x, W_qkv, b_qkv, W_gate, b_gate, W_experts, b_experts):
        import jax, jax.numpy as jnp
        import numpy as np
        NUM_HEADS = 16
        TOP_K = 2
        B, S, D = x.shape
        H = NUM_HEADS
        hd = D // H
        E = W_gate.shape[-1]
        qkv = (x @ W_qkv + b_qkv).reshape(B, S, 3, H, hd)
        q, k, v = (qkv[:, :, 0], qkv[:, :, 1], qkv[:, :, 2])
        attn = jnp.einsum('bqhd,bkhd->bhqk', q, k) / jnp.sqrt(jnp.asarray(hd, x.dtype))
        attn = jax.nn.softmax(attn, axis=-1)
        attn_out = jnp.einsum('bhqk,bkhd->bqhd', attn, v).reshape(B, S, D)
        gate = jax.nn.softmax(x @ W_gate + b_gate, axis=-1)
        top_g, top_i = jax.lax.top_k(gate, TOP_K)
        combine = jnp.sum(jax.nn.one_hot(top_i, E, dtype=x.dtype) * top_g[..., None], axis=2)
        expert_out = jnp.einsum('bsd,edf->bsef', x, W_experts) + b_experts
        moe_out = jnp.einsum('bsef,bse->bsf', expert_out, combine)
        return attn_out + moe_out
    x = _layernorm(x + _L0_attn_ref(x, L0_attn_Wk, L0_attn_bk, L0_attn_Wv, L0_attn_bv, L0_attn_Wq, L0_attn_bq, L0_attn_Wo, L0_attn_bo), axis=-1)
    x = _layernorm(x + _L0_xattn_ref(x, ctx_1024, ctx_1024, L0_xattn_w_q, L0_xattn_b_q, L0_xattn_w_k, L0_xattn_b_k, L0_xattn_w_v, L0_xattn_b_v, L0_xattn_w_o, L0_xattn_b_o), axis=-1)
    x = _layernorm(x + _L0_ffn_ref(x, L0_ffn_W_qkv, L0_ffn_b_qkv, L0_ffn_W_gate, L0_ffn_b_gate, L0_ffn_W_experts, L0_ffn_b_experts), axis=-1)
    return x

_drawn_inputs = setup_inputs


def setup_inputs(seed=0):
    import zlib

    import numpy as np

    out = dict(_drawn_inputs(seed))
    spreads = {'L0_attn_bk': (0.0, 0.1),
     'L0_attn_bv': (0.0, 0.1),
     'L0_attn_bq': (0.0, 0.359),
     'L0_attn_bo': (0.0, 0.1),
     'L0_xattn_b_q': (0.0, 0.8),
     'L0_xattn_b_k': (0.0, 0.8),
     'L0_xattn_b_v': (0.0, 0.1),
     'L0_xattn_b_o': (0.0, 0.1),
     'L0_ffn_b_qkv': (0.0, 0.1),
     'L0_ffn_b_gate': (0.0, 0.1),
     'L0_ffn_b_experts': (0.0, 0.327)}
    factors = {'L0_xattn_w_q': 8.0, 'L0_xattn_w_k': 8.0}
    for name, (base, spread) in spreads.items():
        noise = np.random.default_rng([zlib.crc32(name.encode()), seed]).standard_normal(out[name].shape)
        drawn = base * np.exp(spread * noise) if base else spread * noise
        out[name] = jnp.asarray(drawn.astype(out[name].dtype))
    for name, factor in factors.items():
        out[name] = (out[name] * factor).astype(out[name].dtype)
    return out
```

```python
from contextlib import ExitStack

import concourse.bass as bass
from concourse import mybir

F32 = mybir.dt.float32
BF16 = mybir.dt.bfloat16
I32 = mybir.dt.int32
ALU = mybir.AluOpType
ACT = mybir.ActivationFunctionType
AX_X = mybir.AxisListType.X

P = 128
B, T, D = 8, 512, 256
DC = D // P
TB = T // P
MEM = 128
H, HD = 16, 16
G, HG = 4, 4
E = 8
TERMS = 6
ROWS = TERMS * HD
SHIFT = 2
Q_PART = (0, 0, 1, 0, 2, 1)
K_PART = (0, 1, 0, 2, 0, 1)
EPS = 1e-5
DECAY, RATE = 0.99, 0.01
LAYERS = 2

STEPS = G * TB
MAXES = H * TB
LEAD = 24

MOE_TILES = TB * E // 2
MOE_BANK = [4, 2, 3, 0, 1, 4, 2, 3] + [4] * (MOE_TILES - 8)
MOE_EARLY = 8


def ring_order():
    order = [("max", n) for n in range(HG * TB)] + [("shift", 0)]
    order += [("max", n) for n in range(HG * TB, LEAD)]
    for s in range(STEPS):
        if s % TB == TB - 1 and s + 1 < STEPS:
            order.append(("shift", (s + 1) // TB))
        order += [("max", n) for n in range(LEAD + 4 * s, min(MAXES, LEAD + 4 * s + 4))]
        if s % TB == 1 and s > TB:
            order.append(("heads", s // TB - 1))
    order.append(("heads", G - 1))
    return order


RING = ring_order()
RING_AT = {tile: n for n, tile in enumerate(RING)}


class Signal:

    def __init__(self, ctx, nc, name, per_batch, unit=1, start=0):
        self.sem = ctx.enter_context(nc.semaphore(name))
        self.per_batch, self.unit, self.start = per_batch, unit, start

    def after(self, b, n):
        return b * (self.per_batch * self.unit) + (n * self.unit + self.start)

    def prime(self, eng):
        eng.sem_inc(self.sem, self.start)


def decoder(nc, x, xT, ctxT, w, out):
    with ExitStack() as ctx:
        def sb(name, shape, dt=F32):
            return ctx.enter_context(nc.sbuf_tensor(name, shape, dt))

        def sig(name, per_batch, unit=1, start=0):
            return Signal(ctx, nc, name, per_batch, unit, start)

        W = {name: sb("w_" + name, list(ap.shape)) for name, ap in w.items()}
        ident = W["ident"]
        identb = sb("identb", [P, P], BF16)
        bq2 = sb("bq2s", [P, DC])
        bq3 = sb("bq3s", [P, DC])

        x_s = sb("x_s", [P, TB, D])
        xT_s = sb("xT_s", [P, DC, T])
        ctxT_s = sb("ctxT_s", [P, DC, T])
        q1T = sb("q1T", [P, T])
        k1T = sb("k1T", [P, T])
        v1 = sb("v1", [P, TB, MEM])
        a1 = sb("a1", [P, 4 * T - 768])
        A_AT = [0, 512, 896, 1152]
        o1T = sb("o1T", [P, T])
        res = sb("res", [P, TB, D])
        x1 = sb("x1", [P, TB, D])
        x1T = sb("x1T", [P, DC, T])
        x2 = sb("x2", [P, TB, D])
        x2T = sb("x2T", [P, DC, T])
        y = sb("y", [P, TB, D])
        part_f = {n: sb(n + "_f", [P, DC, T]) for n in "qk"}
        part_r = {n: sb(n + "_r", [P, T]) for n in "qk"}
        part = {n: sb(n + "_parts", [P, DC, 3, T], BF16) for n in "qk"}
        qs = sb("qs", [P, H, T], BF16)
        ks = sb("ks", [P, H, T], BF16)
        v2 = sb("v2", [P, TB, H, 32])
        probs = sb("probs", [P, 2, HG, T])
        oT = sb("oT", [P, T])
        heads = sb("heads", [P, TB, D])
        headsT = sb("headsT", [P, DC, T])
        maxes = sb("maxes", [P, MAXES])
        shift_n = sb("shift_n", [P, G, SHIFT * HG * TB], BF16)
        shift_r = sb("shift_r", [SHIFT * HG * TB, G, P], BF16)
        rsum = sb("rsum", [P, 2, TB, HG])
        stats = sb("stats", [P, TB, 6])
        mv = sb("mv", [P, TB, 2])
        var = sb("var", [P, TB])
        seed = sb("seed", [P, TB], I32)
        rstd_i = sb("rstd_i", [P, TB], I32)
        rstd = sb("rstd", [P, 4, TB])
        newton = sb("newton", [P, 2, TB])
        g_l = sb("g_l", [P, TB, E])
        g_m = sb("g_m", [P, TB])
        g_e = sb("g_e", [P, TB, E])
        g_s = sb("g_s", [P, 2, TB])
        g_p = sb("g_p", [P, TB, E])
        above = sb("above", [P, TB, E, E])
        tied = sb("tied", [P, TB, E, E])
        rank = sb("rank", [P, TB, E])
        comb = sb("comb", [P, TB, P])
        combT = sb("combT", [P, T])
        moe = sb("moe", [P, 4, 512])

        sc = ctx.enter_context(nc.psum_tensor("sc", [P, 4, 512], F32))
        mx = ctx.enter_context(nc.psum_tensor("mx", [P, 2, 512], F32))
        op = ctx.enter_context(nc.psum_tensor("op", [P, 512], F32))
        ms = ctx.enter_context(nc.psum_tensor("ms", [P, 512], F32))

        w_in = sig("w_in", 0, 16)
        const = sig("const", 0)
        fills = sig("fills", 0)
        x_in = sig("x_in", 1, 16)
        xT_in = sig("xT_in", 1, 16)
        ctx_in = sig("ctx_in", 1, 16)
        y_out = sig("y_out", 1, 16, start=1)
        stack_in = [sig(f"stack_in{c}", LAYERS * 2 * TERMS, 16, start=1) for c in range(DC)]
        shift_in = sig("shift_in", LAYERS * G, 16)
        proj1 = sig("proj1", 3, start=1)
        projc = sig("projc", 4, start=1)
        lin_s = sig("lin_s", 3)
        lin_o = sig("lin_o", 1)
        lin_y = sig("lin_y", 2)
        xt = sig("xt", 2 * DC)
        projq = sig("projq", DC)
        ring = sig("ring", LAYERS * len(RING))
        score = sig("score", LAYERS * STEPS * 2, start=1)
        pv = sig("pv", LAYERS * STEPS, start=1)
        ht = sig("ht", DC)
        cross_y = sig("cross_y", 2)
        proj3 = sig("proj3", 2 * DC)
        proj3v = sig("proj3v", 2)
        gate = sig("gate", 1)
        cT = sig("cT", 1)
        moe_b = sig("moe_b", 2)
        moe_t = sig("moe_t", MOE_TILES)
        qk1_out = sig("qk1_out", 2)
        kc_out = sig("kc_out", 2 * DC)
        o1_out = sig("o1_out", 1)
        xt_out = sig("xt_out", 2 * DC)
        qc_out = sig("qc_out", 2 * DC)
        exp_out = sig("exp_out", LAYERS * STEPS * 2, start=1)
        oT_out = sig("oT_out", LAYERS * G, start=1)
        ht_out = sig("ht_out", DC)
        qk3_out = sig("qk3_out", 4 * DC)
        g_exp = sig("g_exp", 1)
        cT_out = sig("cT_out", 1)
        moe_b_out = sig("moe_b_out", 2)
        moe_out = sig("moe_out", 2 * MOE_TILES, start=1)
        v1_out = sig("v1_out", 1)
        a1_out = sig("a1_out", TB)
        vc_out = sig("vc_out", 2)
        res_out = sig("res_out", 3 * 2, start=1)
        ln_step = sig("ln_step", 3 * (4 + 4 + 3 + 9))
        ln_out = sig("ln_out", 3 * TB)
        q_step = sig("q_step", 2 * DC * 3)
        k_step = sig("k_step", 2 * DC * 3)
        ring_out = sig("ring_out", LAYERS * len(RING), start=1)
        shift_cut = sig("shift_cut", LAYERS * G * SHIFT)
        rs = sig("rs", LAYERS * G)
        v3_out = sig("v3_out", 2)
        g_step = sig("g_step", 12)
        xb_out = sig("xb_out", 1)
        x1b_out = sig("x1b_out", 1)
        acc = sig("acc", 2 + 2 * MOE_TILES, start=1)
        lone = {e: sig("lone_" + e, 0) for e in ("sp", "pool", "dve")}

        NW = len(w)
        block = ctx.enter_context(nc.Block())

        def stand(eng, name):
            eng.sem_inc(lone[name].sem, 1)

        @block.sync
        def _(sp):
            for signal in (*stack_in, y_out):
                signal.prime(sp)
            for name, ap in w.items():
                sp.dma_start(W[name][:], ap).then_inc(w_in.sem, 16)
            with sp.Fori(0, B) as b:
                sp.wait_ge(proj1.sem, proj1.after(b, 0))
                stand(sp, "sp")
                sp.dma_start(xT_s[:], xT[bass.ds(b, 1)].rearrange("o (c p) t -> p (o c) t", p=P)).then_inc(xT_in.sem, 16)
                sp.wait_ge(projc.sem, projc.after(b, 0))
                stand(sp, "sp")
                sp.dma_start(ctxT_s[:], ctxT[bass.ds(b, 1)].rearrange("o (c p) t -> p (o c) t", p=P)).then_inc(ctx_in.sem, 16)
                sp.wait_ge(res_out.sem, res_out.after(b, 0))
                stand(sp, "sp")
                sp.dma_start(x_s[:], x[bass.ds(b, 1)].rearrange("o (n p) d -> p (o n) d", p=P)).then_inc(x_in.sem, 16)

                def stack(layer, name, c, dst, which):
                    for r in range(TERMS):
                        sp.dma_start(dst[HD * r:HD * r + HD, 8 * c:8 * c + 8, :], part[name][:, c, which[r], :]) \
                            .then_inc(stack_in[c].sem, 16)

                def shifts(layer):
                    for g in range(G):
                        n = layer * len(RING) + RING_AT["shift", g] + 1
                        sp.wait_ge(ring_out.sem, ring_out.after(b, n))
                        stand(sp, "sp")
                        sp.dma_start(qs[ROWS:ROWS + SHIFT, HG * g:HG * g + HG, :].rearrange("a h (n t) -> a (h n) t", n=TB),
                                     shift_r[:, g, :]).then_inc(shift_in.sem, 16)

                for layer in range(LAYERS):
                    for c in range(DC):
                        if layer == 0:
                            sp.wait_ge(score.sem, score.after(b, 0))
                            stand(sp, "sp")
                        sp.wait_ge(k_step.sem, k_step.after(b, layer * DC * 3 + 3 * c + 3))
                        stand(sp, "sp")
                        stack(layer, "k", c, ks, K_PART)
                        sp.wait_ge(q_step.sem, q_step.after(b, layer * DC * 3 + 3 * c + 3))
                        stand(sp, "sp")
                        stack(layer, "q", c, qs, Q_PART)
                    shifts(layer)
                sp.wait_ge(ln_out.sem, ln_out.after(b, 3 * TB))
                stand(sp, "sp")
                sp.dma_start(out[bass.ds(b, 1)].rearrange("o (n p) d -> p (o n) d", p=P), y[:]).then_inc(y_out.sem, 16)
            sp.wait_ge(y_out.sem, 16 * B + 1)

        @block.tensor
        def _(pe):
            def mm(dst, lhsT, rhs, first, last):
                return nc.tensor.matmul(dst, lhsT, rhs, start=first, stop=last, skip_group_check=True)

            def project(dst, wt, src, cols):
                for c in range(DC):
                    last = mm(dst, wt[:, c, cols], src[:, c, :], c == 0, c == DC - 1)
                return last

            def project_rows(bank, width, src, wt, cols, blocks):
                for j, t in enumerate(blocks):
                    for c in range(DC):
                        last = mm(bank[:, j * width:(j + 1) * width], src[:, c, t * P:(t + 1) * P], wt[:, c, cols],
                                  c == 0, c == DC - 1)
                return last

            def transpose_rows(bank, src, c):
                for t in range(TB):
                    last = nc.tensor.transpose(bank[:, t * P:(t + 1) * P], src[:, t, c * P:(c + 1) * P], ident[:])
                return last

            for signal in (proj1, projc, score, pv):
                signal.prime(pe)
            pe.wait_ge(w_in.sem, 16 * NW)
            pe.wait_ge(const.sem, 3)
            pe.wait_ge(fills.sem, 3)
            with pe.Fori(0, B) as b:
                pe.wait_ge(xT_in.sem, xT_in.after(b, 1))
                pe.wait_ge(exp_out.sem, exp_out.after(b, 0))
                pe.wait_ge(moe_out.sem, moe_out.after(b, 0))
                project(sc[:, 0, :], W["wq1"], xT_s, slice(0, MEM)).then_inc(proj1.sem, 1)
                project(sc[:, 1, :], W["wk1"], xT_s, slice(0, MEM)).then_inc(proj1.sem, 1)
                project_rows(sc[:, 2, :], MEM, xT_s, W["wv1"], slice(0, MEM), range(TB)).then_inc(proj1.sem, 1)
                pe.wait_ge(ctx_in.sem, ctx_in.after(b, 1))
                pe.wait_ge(ring_out.sem, ring_out.after(b, 0))
                for c in range(DC):
                    project(mx[:, c, :], W["wk2"], ctxT_s, slice(c * P, c * P + P)).then_inc(projc.sem, 1)
                pe.wait_ge(qk1_out.sem, qk1_out.after(b, 2))
                spot = [sc[:, 3, 0:512], sc[:, 0, 0:384], sc[:, 1, 0:256], sc[:, 1, 256:384]]
                for i in range(TB):
                    last = mm(spot[i], k1T[:, i * P:i * P + P], q1T[:, i * P:T], True, True)
                    if i != 2:
                        last.then_inc(lin_s.sem, 1)
                project_rows(ms[:, :], D, ctxT_s, W["wv2"], slice(0, D), (0, 1)).then_inc(projc.sem, 1)
                pe.wait_ge(v1_out.sem, v1_out.after(b, 1))
                project_rows(sc[:, 2, :], D, ctxT_s, W["wv2"], slice(0, D), (2, 3)).then_inc(projc.sem, 1)
                pe.wait_ge(oT_out.sem, oT_out.after(b, 0))
                pe.wait_ge(a1_out.sem, a1_out.after(b, TB))
                for i in range(TB):
                    last = mm(op[:, i * P:T], v1[:, i, :], a1[:, A_AT[i]:A_AT[i] + T - i * P], i == 0, i == TB - 1)
                last.then_inc(lin_o.sem, 1)
                pe.wait_ge(kc_out.sem, kc_out.after(b, 2 * DC))
                pe.wait_ge(o1_out.sem, o1_out.after(b, 1))
                for t in range(TB):
                    last = mm(mx[:, t // 2, (t % 2) * D:(t % 2) * D + D], o1T[:, t * P:t * P + P], W["wo1"][:], True, True)
                    if t % 2:
                        last.then_inc(lin_y.sem, 1)
                pe.wait_ge(vc_out.sem, vc_out.after(b, 2))
                pe.wait_ge(ln_out.sem, ln_out.after(b, TB))
                for c in range(DC):
                    transpose_rows(sc[:, 2 + c, :], x1, c).then_inc(xt.sem, 1)
                pe.wait_ge(xt_out.sem, xt_out.after(b, DC))
                for c in range(DC):
                    project(sc[:, c, :], W["wq2"], x1T, slice(c * P, c * P + P)).then_inc(projq.sem, 1)

                def attention(layer):
                    base = layer * len(RING)

                    def ring_tile(kind, n):
                        at = RING_AT[kind, n]
                        slot = at % 2
                        if at >= 2:
                            pe.wait_ge(ring_out.sem, ring_out.after(b, base + at - 1))
                        if kind == "max":
                            h, t = n // TB, n % TB
                            if n % (H // DC * TB) == 0:
                                c = n // (H // DC * TB)
                                pe.wait_ge(stack_in[c].sem, stack_in[c].after(b, (layer + 1) * 2 * TERMS))
                            last = mm(mx[:, slot, :], qs[0:ROWS, h, t * P:t * P + P], ks[0:ROWS, h, :], True, True)
                        elif kind == "shift":
                            pe.wait_ge(shift_cut.sem, shift_cut.after(b, (layer * G + n + 1) * SHIFT))
                            last = nc.tensor.transpose(mx[0:SHIFT * HG * TB, slot, 0:P // 2].bitcast(BF16),
                                                       shift_n[:, n, :], identb[:])
                        else:
                            pe.wait_ge(oT_out.sem, oT_out.after(b, layer * G + n + 1))
                            for t in range(TB):
                                last = nc.tensor.transpose(mx[:, slot, t * P:t * P + P], oT[:, t * P:t * P + P], ident[:])
                        last.then_inc(ring.sem, 1)

                    def scores(s, pair):
                        g, kb = s // TB, s % TB
                        if s >= 1:
                            pe.wait_ge(exp_out.sem, exp_out.after(b, (layer * STEPS + s - 1) * 2 + pair + 1))
                        if kb == 0 and pair == 0:
                            pe.wait_ge(shift_in.sem, shift_in.after(b, layer * G + g + 1))
                        for j in range(2):
                            h = HG * g + 2 * pair + j
                            last = mm(sc[:, 2 * pair + j, :], ks[0:ROWS + SHIFT, h, kb * P:kb * P + P],
                                      qs[0:ROWS + SHIFT, h, :], True, True)
                        last.then_inc(score.sem, 1)

                    def values(s):
                        g, kb = s // TB, s % TB
                        pe.wait_ge(exp_out.sem, exp_out.after(b, (layer * STEPS + s + 1) * 2))
                        if kb == 0 and g >= 1:
                            pe.wait_ge(oT_out.sem, oT_out.after(b, layer * G + g))
                        for j in range(HG):
                            last = mm(op[32 * j:32 * j + 32, :], v2[:, kb, HG * g + j, :], probs[:, s % 2, j, :],
                                      kb == 0, kb == TB - 1)
                        last.then_inc(pv.sem, 1)

                    for n in range(HG * TB):
                        ring_tile("max", n)
                        if layer == 1 and n % 2 == 1:
                            mixture(n // 2)
                    ring_tile("shift", 0)
                    for n in range(HG * TB, LEAD):
                        ring_tile("max", n)
                    if layer == 0:
                        pe.wait_ge(qc_out.sem, qc_out.after(b, 2 * DC))
                    else:
                        pe.wait_ge(moe_out.sem, moe_out.after(b, 2 * MOE_EARLY))
                    for s in range(STEPS):
                        if s % TB == TB - 1 and s + 1 < STEPS:
                            ring_tile("shift", (s + 1) // TB)
                        for pair in range(2):
                            scores(s, pair)
                            for n in range(LEAD + 4 * s + 2 * pair, min(MAXES, LEAD + 4 * s + 2 * pair + 2)):
                                ring_tile("max", n)
                        if s >= 1:
                            if s == 1:
                                if layer == 0:
                                    pe.wait_ge(vc_out.sem, vc_out.after(b, 2))
                                else:
                                    pe.wait_ge(v3_out.sem, v3_out.after(b, 2))
                            values(s - 1)
                        if s % TB == 1 and s > TB:
                            ring_tile("heads", s // TB - 1)
                        if layer == 1 and s % 2 == 0:
                            mixture(MOE_EARLY + s // 2)
                    values(STEPS - 1)
                    ring_tile("heads", G - 1)

                def mixture(n):
                    t, pair = n // (E // 2), n % (E // 2)
                    bank = ms[:, :] if MOE_BANK[n] == 4 else sc[:, MOE_BANK[n], :]
                    before = [m for m in range(n) if MOE_BANK[m] == MOE_BANK[n]]
                    if before:
                        pe.wait_ge(moe_out.sem, moe_out.after(b, 2 * (before[-1] + 1)))
                    elif MOE_BANK[n] == 4:
                        pe.wait_ge(moe_b_out.sem, moe_b_out.after(b, 2))
                    else:
                        pe.wait_ge(qk3_out.sem, qk3_out.after(b, 4 * DC))
                        pe.wait_ge(v3_out.sem, v3_out.after(b, 2))
                    for c in range(DC):
                        last = mm(bank, x2T[:, c, t * P:t * P + P], W["we"][:, c, 2 * pair * D:2 * pair * D + 2 * D],
                                  c == 0, c == DC - 1)
                    last.then_inc(moe_t.sem, 1)

                pe.wait_ge(res_out.sem, res_out.after(b, 2))
                attention(0)
                pe.wait_ge(ring_out.sem, ring_out.after(b, len(RING)))
                for c in range(DC):
                    transpose_rows(sc[:, c, :], heads, c).then_inc(ht.sem, 1)
                pe.wait_ge(ht_out.sem, ht_out.after(b, DC))
                for h in range(2):
                    project_rows(mx[:, h, :], D, headsT, W["wo2"], slice(0, D), (2 * h, 2 * h + 1)).then_inc(cross_y.sem, 1)
                pe.wait_ge(ln_out.sem, ln_out.after(b, 2 * TB))
                for c in range(DC):
                    transpose_rows(sc[:, 2 + c, :], x2, c).then_inc(xt.sem, 1)
                pe.wait_ge(xt_out.sem, xt_out.after(b, 2 * DC))
                w3 = W["wqkv3"]
                for n, bank in enumerate((sc[:, 0, :], sc[:, 1, :], op[:, :], ms[:, :])):
                    c, k = n // 2, n % 2
                    project(bank, w3, x2T, slice(k * D + c * P, k * D + c * P + P)).then_inc(proj3.sem, 1)
                project_rows(mx[:, 0, 0:TB * E], E, x2T, W["wg"], slice(0, E), range(TB)).then_inc(gate.sem, 1)
                for h in range(2):
                    project_rows(sc[:, 2 + h, :], D, x2T, w3, slice(2 * D, 3 * D), (2 * h, 2 * h + 1)).then_inc(proj3v.sem, 1)
                pe.wait_ge(qk3_out.sem, qk3_out.after(b, 4 * DC))
                pe.wait_ge(g_step.sem, g_step.after(b, 12))
                for t in range(TB):
                    last = nc.tensor.transpose(ms[:, t * P:t * P + P], comb[:, t, :], ident[:])
                last.then_inc(cT.sem, 1)
                pe.wait_ge(cT_out.sem, cT_out.after(b, 1))
                for h in range(2):
                    if h == 1:
                        pe.wait_ge(moe_b_out.sem, moe_b_out.after(b, 1))
                    for j in range(2):
                        t = 2 * h + j
                        last = mm(ms[:, j * D:j * D + D], combT[:, t * P:t * P + P], W["be"][:], True, True)
                    last.then_inc(moe_b.sem, 1)
                attention(1)

        @block.scalar
        def _(act):
            def copy(dst, src, bias=None, scale=1.0):
                if bias is None:
                    return nc.scalar.activation(dst, src, ACT.Copy)
                return nc.scalar.activation(dst, src, ACT.Identity, bias=bias, scale=scale)

            for signal in (exp_out, moe_out, oT_out):
                signal.prime(act)
            act.wait_ge(w_in.sem, 16 * NW)
            nc.scalar.mul(bq2[:], W["bq2"][:], HD ** -0.5).then_inc(const.sem, 1)
            nc.scalar.mul(bq3[:], W["bq3"][:], HD ** -0.5).then_inc(const.sem, 1)
            nc.scalar.copy(identb[:], ident[:]).then_inc(const.sem, 1)
            act.wait_ge(const.sem, 3)
            with act.Fori(0, B) as b:
                for n, (dst, bias) in enumerate(((q1T, "bq1"), (k1T, "bk1"))):
                    act.wait_ge(proj1.sem, proj1.after(b, n + 1))
                    copy(dst[:], sc[:, n, :], W[bias][:, 0:1]).then_inc(qk1_out.sem, 1)

                def cut(name, c, bank, bias, scale, done):
                    copy(part_f[name][:, c, :], bank, bias[:, c:c + 1], scale).then_inc(done.sem, 1)
                    copy(part[name][:, c, 0, :], bank, bias[:, c:c + 1], scale).then_inc(done.sem, 1)

                for c in range(DC):
                    act.wait_ge(stack_in[c].sem, stack_in[c].after(b, 0))
                for c in range(DC):
                    act.wait_ge(projc.sem, projc.after(b, c + 1))
                    cut("k", c, mx[:, c, :], W["bk2"], 1.0, kc_out)
                act.wait_ge(lin_o.sem, lin_o.after(b, 1))
                copy(o1T[:], op[:]).then_inc(o1_out.sem, 1)
                for c in range(DC):
                    act.wait_ge(xt.sem, xt.after(b, c + 1))
                    copy(x1T[:, c, :], sc[:, 2 + c, :]).then_inc(xt_out.sem, 1)
                for c in range(DC):
                    act.wait_ge(projq.sem, projq.after(b, c + 1))
                    cut("q", c, sc[:, c, :], bq2, HD ** -0.5, qc_out)

                def exps(layer, s):
                    for pair in range(2):
                        act.wait_ge(score.sem, score.after(b, (layer * STEPS + s) * 2 + pair + 1))
                        if pair == 0:
                            if s >= 2:
                                act.wait_ge(pv.sem, pv.after(b, layer * STEPS + s - 1))
                            else:
                                act.wait_ge(pv.sem, pv.after(b, layer * STEPS))
                        nc.scalar.activation(probs[:, s % 2, 2 * pair:2 * pair + 2, :], sc[:, 2 * pair:2 * pair + 2, :],
                                             ACT.Exp).then_inc(exp_out.sem, 1)

                def group_out(layer, g):
                    act.wait_ge(pv.sem, pv.after(b, layer * STEPS + TB * g + TB))
                    if g >= 1:
                        act.wait_ge(ring.sem, ring.after(b, layer * len(RING) + RING_AT["heads", g - 1] + 1))
                    copy(oT[:], op[:]).then_inc(oT_out.sem, 1)

                def mixture(n):
                    t, pair = n // (E // 2), n % (E // 2)
                    bank = ms[:, :] if MOE_BANK[n] == 4 else sc[:, MOE_BANK[n], :]
                    act.wait_ge(moe_t.sem, moe_t.after(b, n + 1))
                    if n >= 4:
                        act.wait_ge(acc.sem, acc.after(b, 2 + 2 * (n - 3)))
                    else:
                        act.wait_ge(acc.sem, acc.after(b, 2))
                    for j in range(2):
                        e = 2 * pair + j
                        nc.scalar.activation(moe[:, n % 4, j * D:j * D + D], bank[:, j * D:j * D + D], ACT.Copy,
                                             scale=comb[:, t, e:e + 1]).then_inc(moe_out.sem, 1)

                for s in range(STEPS):
                    exps(0, s)
                    if s % TB == 0 and s >= 1:
                        group_out(0, s // TB - 1)
                group_out(0, G - 1)
                for c in range(DC):
                    act.wait_ge(ht.sem, ht.after(b, c + 1))
                    copy(headsT[:, c, :], sc[:, c, :]).then_inc(ht_out.sem, 1)
                for c in range(DC):
                    act.wait_ge(xt.sem, xt.after(b, DC + c + 1))
                    copy(x2T[:, c, :], sc[:, 2 + c, :]).then_inc(xt_out.sem, 1)
                for n, bank in enumerate((sc[:, 0, :], sc[:, 1, :], op[:, :], ms[:, :])):
                    c = n // 2
                    act.wait_ge(stack_in[c].sem, stack_in[c].after(b, 2 * TERMS))
                    act.wait_ge(proj3.sem, proj3.after(b, n + 1))
                    if n % 2 == 0:
                        cut("q", c, bank, bq3, HD ** -0.5, qk3_out)
                    else:
                        cut("k", c, bank, W["bk3"], 1.0, qk3_out)
                act.wait_ge(g_step.sem, g_step.after(b, 3))
                nc.scalar.activation(g_e[:], g_l[:], ACT.Exp).then_inc(g_exp.sem, 1)
                act.wait_ge(cT.sem, cT.after(b, 1))
                copy(combT[:], ms[:]).then_inc(cT_out.sem, 1)
                for h in range(2):
                    act.wait_ge(moe_b.sem, moe_b.after(b, h + 1))
                    act.wait_ge(acc.sem, acc.after(b, 0))
                    copy(moe[:, h, :], ms[:]).then_inc(moe_b_out.sem, 1)
                for n in range(MOE_EARLY):
                    mixture(n)
                for s in range(STEPS):
                    exps(1, s)
                    if s % TB == 0 and s >= 1:
                        group_out(1, s // TB - 1)
                    if s % 2 == 0:
                        mixture(MOE_EARLY + s // 2)
                group_out(1, G - 1)

        @block.vector
        def _(dve):
            for signal in (ring_out, res_out):
                signal.prime(dve)
            dve.wait_ge(w_in.sem, 16 * NW)
            nc.vector.memset(v2[:, :, :, HD:32], 1.0).then_inc(fills.sem, 1)
            nc.vector.memset(ks[ROWS:P, :, :], 1.0).then_inc(fills.sem, 1)
            nc.vector.memset(comb[:], 0.0).then_inc(fills.sem, 1)
            dve.wait_ge(fills.sem, 3)
            with dve.Fori(0, B) as b:
                dve.wait_ge(proj1.sem, proj1.after(b, 3))
                nc.vector.tensor_tensor(v1[:], sc[:, 2, :].rearrange("p (n m) -> p n m", n=TB),
                                        W["bv1"][:].rearrange("p (o m) -> p o m", o=1).broadcast_to([P, TB, MEM]),
                                        ALU.add).then_inc(v1_out.sem, 1)
                spot = [sc[:, 3, 0:512], sc[:, 0, 0:384], sc[:, 1, 0:256], sc[:, 1, 256:384]]
                for i in range(TB):
                    dve.wait_ge(lin_s.sem, lin_s.after(b, min(i + 1, 3)))
                    n = T - i * P
                    nc.vector.tensor_tensor(a1[:, A_AT[i]:A_AT[i] + n], spot[i], W["decay"][:, 0:n], ALU.mult) \
                        .then_inc(a1_out.sem, 1)

                def values_in(bank, h, bias, signal, done):
                    dve.wait_ge(signal.sem, signal.after(b, done))
                    return nc.vector.tensor_tensor(
                        v2[:, 2 * h:2 * h + 2, :, 0:HD], bank.rearrange("p (n h d) -> p n h d", n=2, h=H),
                        bias[:].rearrange("p (o h d) -> p o h d", o=1, h=H).broadcast_to([P, 2, H, HD]), ALU.add)

                for h, bank in enumerate((ms[:, :], sc[:, 2, :])):
                    values_in(bank, h, W["bv2"], projc, DC + h + 1).then_inc(vc_out.sem, 1)

                def layer_norm(k, dst):
                    base = k * (4 + 4 + 3 + 9)
                    for t in range(TB):
                        dve.wait_ge(res_out.sem, res_out.after(b, 2 * k + t // 2 + 1))
                        nc.vector.bn_stats(stats[:, t, :], res[:, t, :]).then_inc(ln_step.sem, 1)
                    for t in range(TB):
                        dve.wait_ge(ln_step.sem, ln_step.after(b, base + t + 1))
                        stand(dve, "dve")
                        nc.vector.bn_aggr(mv[:, t, :], stats[:, t, :]).then_inc(ln_step.sem, 1)
                    dve.wait_ge(ln_step.sem, ln_step.after(b, base + 8))
                    nc.vector.tensor_scalar(var[:], mv[:, :, 1], EPS, None, ALU.add).then_inc(ln_step.sem, 1)
                    dve.wait_ge(ln_step.sem, ln_step.after(b, base + 9))
                    nc.vector.tensor_scalar(seed[:], var[:].bitcast(I32), 1, None, ALU.logical_shift_right) \
                        .then_inc(ln_step.sem, 1)
                    dve.wait_ge(ln_step.sem, ln_step.after(b, base + 10))
                    nc.vector.tensor_scalar(rstd_i[:], seed[:], -1.0, float(0x5F3759DF), ALU.mult, ALU.add) \
                        .then_inc(ln_step.sem, 1)
                    guess = rstd_i[:].bitcast(F32)
                    for i in range(3):
                        n = base + 11 + 3 * i
                        dve.wait_ge(ln_step.sem, ln_step.after(b, n))
                        nc.vector.scalar_tensor_tensor(out=newton[:, 0, :], in0=guess, scalar=-0.5, in1=guess,
                                                       op0=ALU.mult, op1=ALU.mult).then_inc(ln_step.sem, 1)
                        dve.wait_ge(ln_step.sem, ln_step.after(b, n + 1))
                        nc.vector.tensor_tensor(newton[:, 1, :], newton[:, 0, :], var[:], ALU.mult) \
                            .then_inc(ln_step.sem, 1)
                        dve.wait_ge(ln_step.sem, ln_step.after(b, n + 2))
                        nc.vector.scalar_tensor_tensor(out=rstd[:, i, :], in0=newton[:, 1, :], scalar=1.5, in1=guess,
                                                       op0=ALU.add, op1=ALU.mult).then_inc(ln_step.sem, 1)
                        guess = rstd[:, i, :]
                    dve.wait_ge(ln_step.sem, ln_step.after(b, base + 20))
                    for t in range(TB):
                        nc.vector.tensor_scalar(dst[:, t, :], res[:, t, :], mv[:, t, 0:1], rstd[:, 2, t:t + 1],
                                                ALU.subtract, ALU.mult).then_inc(ln_out.sem, 1)

                def cut(layer, c, done):
                    n = (layer * DC + c) * 3
                    dve.wait_ge(done.sem, done.after(b, (2 if layer == 0 else 4) * c + 2))
                    if n:
                        dve.wait_ge(q_step.sem, q_step.after(b, n))
                    nc.vector.tensor_tensor(part_r["q"][:], part_f["q"][:, c, :], part["q"][:, c, 0, :], ALU.subtract) \
                        .then_inc(q_step.sem, 1)
                    dve.wait_ge(q_step.sem, q_step.after(b, n + 1))
                    nc.vector.tensor_copy(part["q"][:, c, 1, :], part_r["q"][:]).then_inc(q_step.sem, 1)
                    dve.wait_ge(q_step.sem, q_step.after(b, n + 2))
                    nc.vector.tensor_tensor(part["q"][:, c, 2, :], part_r["q"][:], part["q"][:, c, 1, :], ALU.subtract) \
                        .then_inc(q_step.sem, 1)

                def ring_tile(layer, kind, n):
                    base = layer * len(RING)
                    at = RING_AT[kind, n]
                    slot = at % 2
                    dve.wait_ge(ring.sem, ring.after(b, base + at + 1))
                    if kind == "max":
                        nc.vector.tensor_reduce(maxes[:, n:n + 1], mx[:, slot, :], AX_X, ALU.max) \
                            .then_inc(ring_out.sem, 1)
                        g, size = n // (HG * TB), HG * TB
                        if n % size == size - 1:
                            m = maxes[:, g * size:(g + 1) * size]
                            dve.wait_ge(ring_out.sem, ring_out.after(b, base + at + 1))
                            nc.vector.tensor_scalar(shift_n[:, g, 0:size], m, -1.0, None, ALU.mult) \
                                .then_inc(shift_cut.sem, 1)
                            dve.wait_ge(shift_cut.sem, shift_cut.after(b, (layer * G + g) * SHIFT + 1))
                            nc.vector.scalar_tensor_tensor(out=shift_n[:, g, size:2 * size], in0=m, scalar=-1.0,
                                                           in1=shift_n[:, g, 0:size], op0=ALU.mult,
                                                           op1=ALU.subtract).then_inc(shift_cut.sem, 1)
                    elif kind == "shift":
                        nc.vector.tensor_copy(shift_r[:, n, :], mx[0:SHIFT * HG * TB, slot, 0:P // 2].bitcast(BF16)) \
                            .then_inc(ring_out.sem, 1)
                    else:
                        v = mx[:, slot, :].rearrange("p (n h d) -> p n h d", n=TB, h=HG)
                        nc.vector.reciprocal(rsum[:, n % 2], v[:, :, :, HD]).then_inc(rs.sem, 1)
                        dve.wait_ge(rs.sem, rs.after(b, layer * G + n + 1))
                        dst = heads[:, :, n * HG * HD:(n + 1) * HG * HD].rearrange("p n (h d) -> p n h d", h=HG)
                        nc.vector.tensor_tensor(dst, v[:, :, :, 0:HD],
                                                rsum[:, n % 2].rearrange("p n (h o) -> p n h o", o=1).broadcast_to([P, TB, HG, HD]),
                                                ALU.mult).then_inc(ring_out.sem, 1)

                def attention(layer):
                    for kind, n in RING:
                        ring_tile(layer, kind, n)

                dve.wait_ge(xb_out.sem, xb_out.after(b, 1))
                for h in range(2):
                    dve.wait_ge(lin_y.sem, lin_y.after(b, h + 1))
                    nc.vector.tensor_tensor(res[:, 2 * h:2 * h + 2, :], mx[:, h, :].rearrange("p (n d) -> p n d", n=2),
                                            x_s[:, 2 * h:2 * h + 2, :], ALU.add).then_inc(res_out.sem, 1)
                layer_norm(0, x1)
                for c in range(DC):
                    cut(0, c, qc_out)
                attention(0)
                dve.wait_ge(x1b_out.sem, x1b_out.after(b, 1))
                dve.wait_ge(ln_out.sem, ln_out.after(b, TB))
                for h in range(2):
                    dve.wait_ge(cross_y.sem, cross_y.after(b, h + 1))
                    nc.vector.tensor_tensor(res[:, 2 * h:2 * h + 2, :], mx[:, h, :].rearrange("p (n d) -> p n d", n=2),
                                            x1[:, 2 * h:2 * h + 2, :], ALU.add).then_inc(res_out.sem, 1)
                layer_norm(1, x2)
                cut(1, 0, qk3_out)
                dve.wait_ge(gate.sem, gate.after(b, 1))
                wide = [P, TB, E]

                def g_wait(n):
                    dve.wait_ge(g_step.sem, g_step.after(b, n))

                nc.vector.tensor_tensor(g_p[:], mx[:, 0, 0:TB * E].rearrange("p (n e) -> p n e", n=TB),
                                        W["bg"][:].rearrange("p (o e) -> p o e", o=1).broadcast_to(wide),
                                        ALU.add).then_inc(g_step.sem, 1)
                g_wait(1)
                nc.vector.tensor_reduce(g_m[:], g_p[:], AX_X, ALU.max).then_inc(g_step.sem, 1)
                g_wait(2)
                nc.vector.tensor_tensor(g_l[:], g_p[:], g_m[:].rearrange("p (n o) -> p n o", o=1).broadcast_to(wide),
                                        ALU.subtract).then_inc(g_step.sem, 1)
                dve.wait_ge(g_exp.sem, g_exp.after(b, 1))
                nc.vector.tensor_reduce(g_s[:, 0, :], g_e[:], AX_X, ALU.add).then_inc(g_step.sem, 1)
                g_wait(4)
                nc.vector.reciprocal(g_s[:, 1, :], g_s[:, 0, :]).then_inc(g_step.sem, 1)
                g_wait(5)
                nc.vector.tensor_tensor(g_p[:], g_e[:],
                                        g_s[:, 1, :].rearrange("p (n o) -> p n o", o=1).broadcast_to(wide),
                                        ALU.mult).then_inc(g_step.sem, 1)
                g_wait(6)
                mine = g_p[:].rearrange("p n (e o) -> p n e o", o=1).broadcast_to([P, TB, E, E])
                other = g_p[:].rearrange("p n (o e) -> p n o e", o=1).broadcast_to([P, TB, E, E])
                nc.vector.tensor_tensor(above[:], other, mine, ALU.is_gt).then_inc(g_step.sem, 1)
                nc.vector.tensor_tensor(tied[:], other, mine, ALU.is_equal).then_inc(g_step.sem, 1)
                g_wait(8)
                earlier = W["earlier"][:].rearrange("p (o m) -> p o m", o=1).broadcast_to([P, TB, E * E])
                nc.vector.tensor_tensor(tied[:].rearrange("p n e m -> p n (e m)"),
                                        tied[:].rearrange("p n e m -> p n (e m)"), earlier, ALU.mult) \
                    .then_inc(g_step.sem, 1)
                g_wait(9)
                nc.vector.tensor_tensor(above[:], above[:], tied[:], ALU.add).then_inc(g_step.sem, 1)
                g_wait(10)
                nc.vector.tensor_reduce(rank[:], above[:], AX_X, ALU.add).then_inc(g_step.sem, 1)
                g_wait(11)
                nc.vector.scalar_tensor_tensor(out=comb[:, :, 0:E], in0=rank[:], scalar=2.0, in1=g_p[:],
                                               op0=ALU.is_lt, op1=ALU.mult).then_inc(g_step.sem, 1)
                cut(1, 1, qk3_out)
                for h in range(2):
                    values_in(sc[:, 2 + h, :], h, W["bv3"], proj3v, h + 1).then_inc(v3_out.sem, 1)
                attention(1)
                dve.wait_ge(acc.sem, acc.after(b, 2 + 2 * MOE_TILES))
                dve.wait_ge(ring_out.sem, ring_out.after(b, LAYERS * len(RING)))
                for h in range(2):
                    nc.vector.tensor_tensor(res[:, 2 * h:2 * h + 2, :], heads[:, 2 * h:2 * h + 2, :],
                                            x2[:, 2 * h:2 * h + 2, :], ALU.add).then_inc(res_out.sem, 1)
                dve.wait_ge(y_out.sem, y_out.after(b, 0))
                layer_norm(2, y)

        @block.gpsimd
        def _(pool):
            acc.prime(pool)
            pool.wait_ge(w_in.sem, 16 * NW)
            with pool.Fori(0, B) as b:
                pool.wait_ge(x_in.sem, x_in.after(b, 1))
                nc.gpsimd.tensor_tensor(x_s[:], x_s[:],
                                        W["bo1"][:].rearrange("p (o d) -> p o d", o=1).broadcast_to([P, TB, D]),
                                        ALU.add).then_inc(xb_out.sem, 1)

                def cut(layer, c, done, at):
                    n = (layer * DC + c) * 3
                    pool.wait_ge(done.sem, done.after(b, at))
                    if n:
                        pool.wait_ge(k_step.sem, k_step.after(b, n))
                    nc.gpsimd.tensor_tensor(part_r["k"][:], part_f["k"][:, c, :], part["k"][:, c, 0, :], ALU.subtract) \
                        .then_inc(k_step.sem, 1)
                    pool.wait_ge(k_step.sem, k_step.after(b, n + 1))
                    stand(pool, "pool")
                    nc.gpsimd.tensor_copy(part["k"][:, c, 1, :], part_r["k"][:]).then_inc(k_step.sem, 1)
                    pool.wait_ge(k_step.sem, k_step.after(b, n + 2))
                    nc.gpsimd.tensor_tensor(part["k"][:, c, 2, :], part_r["k"][:], part["k"][:, c, 1, :], ALU.subtract) \
                        .then_inc(k_step.sem, 1)

                for c in range(DC):
                    cut(0, c, kc_out, 2 * c + 2)
                pool.wait_ge(xt.sem, xt.after(b, DC))
                nc.gpsimd.tensor_tensor(x1[:], x1[:],
                                        W["bo2"][:].rearrange("p (o d) -> p o d", o=1).broadcast_to([P, TB, D]),
                                        ALU.add).then_inc(x1b_out.sem, 1)
                for c in range(DC):
                    cut(1, c, qk3_out, 4 * c + 4)
                for h in range(2):
                    pool.wait_ge(moe_b_out.sem, moe_b_out.after(b, h + 1))
                    nc.gpsimd.tensor_tensor(x2[:, 2 * h:2 * h + 2, :], x2[:, 2 * h:2 * h + 2, :],
                                            moe[:, h, :].rearrange("p (n d) -> p n d", n=2), ALU.add).then_inc(acc.sem, 1)
                for n in range(MOE_TILES):
                    t = n // (E // 2)
                    for j in range(2):
                        pool.wait_ge(moe_out.sem, moe_out.after(b, 2 * n + j + 1))
                        pool.wait_ge(acc.sem, acc.after(b, 2 + 2 * n + j))
                        nc.gpsimd.tensor_tensor(x2[:, t, :], x2[:, t, :], moe[:, n % 4, j * D:j * D + D], ALU.add) \
                            .then_inc(acc.sem, 1)


def by_chunk(a):
    return a.reshape(DC, P, -1).transpose(1, 0, 2)


def head_rows(a):
    return a.reshape(DC, H // DC, HD, -1).transpose(0, 2, 1, 3).reshape(D, -1)


def kernel(**inputs):
    import numpy as np
    import concourse.bacc as bacc
    from concourse.bass_utils import run_bass_kernel_spmd as run

    def arr(name):
        return np.asarray(inputs[name])

    def rows(a):
        return np.broadcast_to(a.reshape(1, -1), (P, a.size))

    x, ctx = arr("x"), arr("ctx_1024")
    attn, cross, ffn = "L0_attn_", "L0_xattn_", "L0_ffn_"
    wqkv, bqkv = arr(ffn + "W_qkv"), arr(ffn + "b_qkv")
    lag = np.arange(T)[None, :] - 1 - np.arange(P)[:, None]
    weights = {
        "wq1": by_chunk(arr(attn + "Wq").T), "wk1": by_chunk(arr(attn + "Wk").T), "wv1": by_chunk(arr(attn + "Wv").T),
        "bq1": arr(attn + "bq").reshape(P, 1), "bk1": arr(attn + "bk").reshape(P, 1), "bv1": rows(arr(attn + "bv")),
        "wo1": arr(attn + "Wo").T, "bo1": rows(arr(attn + "bo")),
        "wq2": by_chunk(head_rows(arr(cross + "w_q")).T), "wk2": by_chunk(head_rows(arr(cross + "w_k")).T),
        "wv2": by_chunk(arr(cross + "w_v").T), "wo2": by_chunk(arr(cross + "w_o").T),
        "bq2": head_rows(arr(cross + "b_q")).reshape(DC, P).T, "bk2": head_rows(arr(cross + "b_k")).reshape(DC, P).T,
        "bv2": rows(arr(cross + "b_v")), "bo2": rows(arr(cross + "b_o")),
        "wqkv3": by_chunk(np.concatenate([head_rows(wqkv[:, :D].T).T, head_rows(wqkv[:, D:2 * D].T).T, wqkv[:, 2 * D:]], 1)),
        "bq3": head_rows(bqkv[:D]).reshape(DC, P).T, "bk3": head_rows(bqkv[D:2 * D]).reshape(DC, P).T,
        "bv3": rows(bqkv[2 * D:]),
        "wg": by_chunk(arr(ffn + "W_gate")), "bg": rows(arr(ffn + "b_gate")),
        "we": by_chunk(arr(ffn + "W_experts").transpose(1, 0, 2).reshape(D, E * D)),
        "be": np.concatenate([arr(ffn + "b_experts"), np.zeros((P - E, D), np.float32)], 0),
        "ident": np.eye(P, dtype=np.float32),
        "decay": np.where(lag >= 0, RATE * DECAY ** np.maximum(lag, 0.0), 0.0).astype(np.float32),
        "earlier": rows((np.arange(E)[None, :] < np.arange(E)[:, None]).astype(np.float32)),
    }
    arrays = {"in_x": x, "in_xT": x.transpose(0, 2, 1), "in_ctxT": ctx.transpose(0, 2, 1)}
    arrays.update({"in_" + n: a for n, a in weights.items()})
    arrays = {n: np.ascontiguousarray(a) for n, a in arrays.items()}
    nc = bacc.Bacc("TRN2", target_bir_lowering=False, num_devices=1)
    ap = {n: nc.dram_tensor(n, a.shape, F32, kind="ExternalInput").ap() for n, a in arrays.items()}
    out = nc.dram_tensor("out_0", x.shape, F32, kind="ExternalOutput").ap()
    decoder(nc, ap["in_x"], ap["in_xT"], ap["in_ctxT"], {n: ap["in_" + n] for n in weights}, out)
    r = run(nc, [arrays], core_ids=[0])
    return r.results[0]["out_0"]
```

```python
from contextlib import ExitStack

import concourse.bass as bass
from concourse import mybir

F32 = mybir.dt.float32
BF16 = mybir.dt.bfloat16
I32 = mybir.dt.int32
F32R = mybir.dt.float32r
ALU = mybir.AluOpType
ACT = mybir.ActivationFunctionType
AX_X = mybir.AxisListType.X

P = 128
B, T, D = 8, 512, 256
DC = D // P
TB = T // P
MEM = 128
H, HD = 16, 16
G, HG = 4, 4
E = 8
TERMS = 6
ROWS = TERMS * HD
SHIFT = 2
Q_PART = (0, 0, 1, 0, 2, 1)
K_PART = (0, 1, 0, 2, 0, 1)
EPS = 1e-5
DECAY, RATE = 0.99, 0.01
LAYERS = 2

STEPS = G * TB
MAXES = H * TB
AHEAD = (32, 24)
RESUME = (3, 0)
PER_STEP = (5, 4)
NEXT_STEP = 5
SHIFT_AFTER = {(0, 1): 6, (0, 2): 9}
NEXT_FROM = 10

MOE_TILES = TB * E // 2
MOE_LEAD = 3
MOE_EARLY = 12
MOE_BANK = [3, 5, 0, 1, 2, 4] * 2 + [4] * (MOE_TILES - MOE_EARLY)

BESIDE = ({2: "q1", 3: "k1", 4: "v1", 5: "s0", 6: "s1", 7: "s23", 8: "o1", 9: "y01", 10: "y23", 14: "x0", 15: "x1"},
          {0: "kc0", 1: "qc0", 2: 12, 3: "kc1", 4: "qc1", 5: 13, 7: 14, 9: 15})
NORM_AT = 11


def beside(layer, step, more):
    task = BESIDE[layer].get(step)
    return task if more or isinstance(task, int) else None


def first_tiles(elt, layer):
    size = HG * TB
    late = size + 2
    return [("max", elt, layer, n) for n in range(late)] + [("shift", elt, layer, 0)] + \
           [("max", elt, layer, n) for n in range(late, AHEAD[layer])]


def step_tiles(layer, s, more):
    front, behind = [], []
    if s % TB == TB - 1 and s + 1 < STEPS and (layer, s // TB) not in SHIFT_AFTER:
        front.append(("shift", 0, layer, (s + 1) // TB))
    if more and layer == 1 and s == STEPS - 2:
        front.append(("shift", 1, 0, 0))
    n = AHEAD[layer] + PER_STEP[layer] * (s - RESUME[layer])
    spread = [("max", 0, layer, m) for m in range(n, min(MAXES, n + PER_STEP[layer]))] if s >= RESUME[layer] else []
    for g in range(1, G):
        if SHIFT_AFTER.get((layer, g - 1)) == s:
            spread.append(("shift", 0, layer, g))
    if more and layer == 1 and s >= NEXT_FROM:
        n = NEXT_STEP * (s - NEXT_FROM)
        spread = [("max", 1, 0, m) for m in range(n, n + NEXT_STEP)]
    if s % TB == 1 and s > TB:
        behind.append(("heads", 0, layer, s // TB - 1))
    return front, spread, behind


def tail_tiles(layer, more):
    n = NEXT_STEP * (STEPS - NEXT_FROM)
    spread = [("max", 1, 0, m) for m in range(n, AHEAD[0])] if more and layer == 1 else []
    return spread, [("heads", 0, layer, G - 1)]


def ring_places(more):
    order = []
    for layer in range(LAYERS):
        if layer == 1:
            order += first_tiles(0, 1)
        for s in range(STEPS):
            for tiles in step_tiles(layer, s, more):
                order += tiles
        for tiles in tail_tiles(layer, more):
            order += tiles
    return {tile: n for n, tile in enumerate(order)}


RING = {more: ring_places(more) for more in (False, True)}
RING_FIRST = {tile: n - len(first_tiles(0, 0)) for n, tile in enumerate(first_tiles(1, 0))}
RING_N = len(RING[True])
RING_LEAD = len(first_tiles(0, 0))


SPLIT = 2.0 ** 12 + 1


class Signal:

    def __init__(self, ctx, nc, name, per_batch, unit=1, start=0):
        self.sem = ctx.enter_context(nc.semaphore(name))
        self.per_batch, self.unit, self.start = per_batch, unit, start

    def after(self, b, n):
        return b * (self.per_batch * self.unit) + (n * self.unit + self.start)

    def prime(self, eng):
        eng.sem_inc(self.sem, self.start)


def decoder(nc, x, xT, ctxT, w, out):
    with ExitStack() as ctx:
        def sb(name, shape, dt=F32):
            return ctx.enter_context(nc.sbuf_tensor(name, shape, dt))

        def sig(name, per_batch, unit=1, start=0):
            return Signal(ctx, nc, name, per_batch, unit, start)

        W = {name: sb("w_" + name, list(ap.shape)) for name, ap in w.items() if name != "we"}
        ident = W["ident"]
        identb = sb("identb", [P, P], BF16)
        bq2 = sb("bq2s", [P, DC])
        bq3 = sb("bq3s", [P, DC])

        x_s = sb("x_s", [P, TB, D])
        xT_s = sb("xT_s", [P, DC, T])
        ctxT_s = sb("ctxT_s", [P, DC, T])
        q1T = sb("q1T", [P, T])
        k1T = sb("k1T", [P, T])
        A_AT = [0, 512, 896, 1152]
        o1T = sb("o1T", [P, T])
        res = sb("res", [P, TB, D])
        x1b = sb("x1b", [P, TB, D])
        x1 = sb("x1", [P, TB, D])
        x1T = sb("x1T", [P, DC, T])
        x2 = sb("x2", [P, TB, D])
        x2T = sb("x2T", [P, DC, T])
        y = x1b
        part_f = {"q": x_s[:].rearrange("p n d -> p (n d)").rearrange("p (c t) -> p c t", c=DC), "k": xT_s}
        part_r = {"q": q1T, "k": k1T}
        part = {n: sb(n + "_parts", [P, DC, 3, T], BF16) for n in "qk"}
        qs = sb("qs", [P, H, T], BF16)
        ks = sb("ks", [P, H, T], BF16)
        v2 = [sb(f"v2_{n}", [P, TB, H, 32]) for n in range(LAYERS)]
        probs = sb("probs", [P, 2, HG, T])
        oT = sb("oT", [P, T])
        heads = sb("heads", [P, TB, D])
        headsT = x2T
        maxes = sb("maxes", [P, MAXES])
        shift_n = sb("shift_n", [P, G, SHIFT * HG * TB], BF16)
        shift_r = sb("shift_r", [SHIFT * HG * TB, G, P], BF16)
        rsum = sb("rsum", [P, 2, TB, HG])
        stats = sb("stats", [P, TB, 6])
        mv = sb("mv", [P, TB, 2])
        var = sb("var", [P, TB])
        seed = sb("seed", [P, TB], I32)
        rstd_i = sb("rstd_i", [P, TB], I32)
        rstd = sb("rstd", [P, 4, TB])
        newton = sb("newton", [P, 2, TB])
        g_l = sb("g_l", [P, TB, E])
        g_m = sb("g_m", [P, TB])
        g_e = sb("g_e", [P, TB, E])
        g_s = sb("g_s", [P, 2, TB])
        g_p = sb("g_p", [P, TB, E])
        above = sb("above", [P, TB, E, E])
        tied = sb("tied", [P, TB, E, E])
        rank = sb("rank", [P, TB, E])
        comb = sb("comb", [P, TB, P])
        combT = o1T
        moe = sb("moe", [P, 4, 512])
        v1 = moe[:, 0, :].rearrange("p (n m) -> p n m", n=TB)
        a1 = moe[:, 1:4, :].rearrange("p n m -> p (n m)")
        x2T_part = (sb("x2T_hi", [P, DC, T]), sb("x2T_lo", [P, DC, T]))
        we_part = (sb("we_hi", [P, DC, E * D]), sb("we_lo", [P, DC, E * D]))
        we_all = probs[:].rearrange("p s h t -> p (s h t)").rearrange("p (c n) -> p c n", c=DC)
        x_rest = x1b[:].rearrange("p n d -> p (n d)").rearrange("p (c t) -> p c t", c=DC)
        w_rest = qs[:].bitcast(F32).rearrange("p h t -> p (h t)").rearrange("p (c n) -> p c n", c=DC)

        sc = ctx.enter_context(nc.psum_tensor("sc", [P, 4, 512], F32))
        mx = ctx.enter_context(nc.psum_tensor("mx", [P, 2, 512], F32))
        op = ctx.enter_context(nc.psum_tensor("op", [P, 512], F32))
        ms = ctx.enter_context(nc.psum_tensor("ms", [P, 512], F32))

        w_cut = sig("w_cut", 0)
        x_cut = sig("x_cut", 3)
        w_in = sig("w_in", 0, 16)
        w_late = sig("w_late", 0, 16)
        const = sig("const", 0)
        fills = sig("fills", 0)
        x_in = sig("x_in", 1, 16)
        xT_in = sig("xT_in", 1, 16)
        ctx_in = sig("ctx_in", 1, 16)
        y_out = sig("y_out", 1, 16)
        y_free = sig("y_free", 1, start=1)
        stack_in = [sig(f"stack_in{c}", LAYERS * 2 * TERMS, 16, start=1) for c in range(DC)]
        shift_in = sig("shift_in", LAYERS * G, 16)
        proj1 = sig("proj1", 3)
        projc = sig("projc", 4)
        lin_s = sig("lin_s", 3)
        lin_o = sig("lin_o", 1)
        lin_y = sig("lin_y", 2)
        x1t = sig("x1t", DC)
        x2t = sig("x2t", 1)
        projq = sig("projq", DC)
        ring = sig("ring", RING_N)
        score = sig("score", LAYERS * STEPS * 2, start=1)
        pv = sig("pv", LAYERS * STEPS, start=1)
        ht = sig("ht", DC)
        cross_y = sig("cross_y", 2)
        proj3 = sig("proj3", 2 * DC)
        proj3v = sig("proj3v", 2)
        gate = sig("gate", 1)
        cT = sig("cT", 1)
        moe_b = sig("moe_b", 2)
        moe_t = sig("moe_t", MOE_TILES)
        qk1_out = sig("qk1_out", 2)
        kc_out = sig("kc_out", 2 * DC)
        o1_out = sig("o1_out", 1)
        x1t_out = sig("x1t_out", DC)
        x2t_out = sig("x2t_out", DC)
        qc_out = sig("qc_out", 2 * DC)
        exp_out = sig("exp_out", LAYERS * STEPS * 2, start=1)
        oT_out = sig("oT_out", LAYERS * G, start=1)
        ht_out = sig("ht_out", DC)
        qk3_out = sig("qk3_out", 4 * DC)
        g_exp = sig("g_exp", 1)
        cT_out = sig("cT_out", 1)
        moe_b_out = sig("moe_b_out", 2)
        moe_out = sig("moe_out", 2 * MOE_TILES, start=1)
        v1_out = sig("v1_out", 1)
        a1_out = sig("a1_out", 3)
        vc_out = sig("vc_out", 2)
        res_out = [sig(f"res_out{k}", 2) for k in range(3)]
        ln_step = [sig(f"ln_step{k}", 4 + 4 + 3 + 9) for k in range(3)]
        ln_out = [sig(f"ln_out{k}", TB) for k in range(3)]
        q_step = sig("q_step", 2 * DC * 3)
        k_step = sig("k_step", 2 * DC * 3)
        ring_out = sig("ring_out", RING_N)
        shift_cut = sig("shift_cut", LAYERS * G * SHIFT)
        rs = sig("rs", LAYERS * G)
        v3_out = sig("v3_out", 2)
        g_step = sig("g_step", 12)
        xb_out = sig("xb_out", 1)
        x1b_out = sig("x1b_out", 1)
        acc = sig("acc", 2 + 2 * MOE_TILES, start=1)
        lone = {e: sig("lone_" + e, 0) for e in ("sp", "pool", "dve")}

        EARLY = ("wq1", "wk1", "wv1", "bq1", "bk1", "bv1", "wo1", "bo1", "decay", "ident")
        LATE = tuple(n for n in w if n not in EARLY)
        QK3_BANK = (sc[:, 2, :], sc[:, 3, :], op[:], sc[:, 0, :])
        V2_BANK = (ms[:], op[:])
        block = ctx.enter_context(nc.Block())

        def stand(eng, name):
            eng.sem_inc(lone[name].sem, 1)

        def ring_at(tile, more):
            return RING_LEAD + (RING_FIRST if more is None else RING[more])[tile]


        @block.sync
        def _(sp):
            def load(n, guard):
                if guard:
                    sp.wait_ge(proj1.sem, proj1.after(n - 1, 3))
                    stand(sp, "sp")
                sp.dma_start(xT_s[:], xT[bass.ds(n, 1)].rearrange("o (c p) t -> p (o c) t", p=P)).then_inc(xT_in.sem, 16)
                if guard:
                    sp.wait_ge(res_out[0].sem, res_out[0].after(n - 1, 2))
                    stand(sp, "sp")
                sp.dma_start(x_s[:], x[bass.ds(n, 1)].rearrange("o (n p) d -> p (o n) d", p=P)).then_inc(x_in.sem, 16)
                if guard:
                    sp.wait_ge(projc.sem, projc.after(n - 1, 4))
                    stand(sp, "sp")
                sp.dma_start(ctxT_s[:], ctxT[bass.ds(n, 1)].rearrange("o (c p) t -> p (o c) t", p=P)).then_inc(ctx_in.sem, 16)

            def stack(n, layer, c):
                for name, dst, which, step in (("k", ks, K_PART, k_step), ("q", qs, Q_PART, q_step)):
                    sp.wait_ge(step.sem, step.after(n, (layer * DC + c) * 3 + 3))
                    stand(sp, "sp")
                    for r in range(TERMS):
                        sp.dma_start(dst[HD * r:HD * r + HD, 8 * c:8 * c + 8, :], part[name][:, c, which[r], :]) \
                            .then_inc(stack_in[c].sem, 16)

            def shift(b, tile, more):
                g = tile[3]
                sp.wait_ge(ring_out.sem, ring_out.after(b, ring_at(tile, more) + 1))
                stand(sp, "sp")
                sp.dma_start(qs[ROWS:ROWS + SHIFT, HG * g:HG * g + HG, :].rearrange("a h (n t) -> a (h n) t", n=TB),
                             shift_r[:, g, :]).then_inc(shift_in.sem, 16)

            def turn(b, more):
                if more:
                    load(b + 1, True)
                for g in range(1, G):
                    shift(b, ("shift", 0, 0, g), more)
                sp.wait_ge(score.sem, score.after(b, STEPS * 2))
                stand(sp, "sp")
                for c in range(DC):
                    stack(b, 1, c)
                for g in range(G - 1):
                    shift(b, ("shift", 0, 1, g), more)
                if more:
                    sp.wait_ge(score.sem, score.after(b, (STEPS + STEPS // 2) * 2))
                    stand(sp, "sp")
                    stack(b + 1, 0, 0)
                shift(b, ("shift", 0, 1, G - 1), more)
                if more:
                    shift(b, ("shift", 1, 0, 0), more)
                    sp.wait_ge(score.sem, score.after(b, 2 * STEPS * 2))
                    stand(sp, "sp")
                    stack(b + 1, 0, 1)

            for signal in stack_in:
                signal.prime(sp)
            for name in ("wq1", "wk1", "ident"):
                sp.dma_start(W[name][:], w[name]).then_inc(w_in.sem, 16)
            load(0, False)
            for name in LATE:
                sp.dma_start(we_all[:] if name == "we" else W[name][:], w[name]).then_inc(w_late.sem, 16)
            for c in range(DC):
                stack(0, 0, c)
            shift(0, ("shift", 1, 0, 0), None)
            with sp.Fori(0, B - 1) as b:
                turn(b, True)
            turn(B - 1, False)

        @block.tensor
        def _(pe):
            def mm(dst, lhsT, rhs, first, last):
                return nc.tensor.matmul(dst, lhsT, rhs, start=first, stop=last, skip_group_check=True)

            def project(dst, wt, src, cols):
                for c in range(DC):
                    last = mm(dst, wt[:, c, cols], src[:, c, :], c == 0, c == DC - 1)
                return last

            def project_rows(bank, width, src, wt, cols, blocks):
                for j, t in enumerate(blocks):
                    for c in range(DC):
                        last = mm(bank[:, j * width:(j + 1) * width], src[:, c, t * P:(t + 1) * P], wt[:, c, cols],
                                  c == 0, c == DC - 1)
                return last

            def transpose_rows(bank, src, c):
                for t in range(TB):
                    last = nc.tensor.transpose(bank[:, t * P:(t + 1) * P], src[:, t, c * P:(c + 1) * P], ident[:])
                return last

            def spare(task, n):
                if task == "q1":
                    pe.wait_ge(xT_in.sem, xT_in.after(n, 1))
                    project(ms[:], W["wq1"], xT_s, slice(0, MEM)).then_inc(proj1.sem, 1)
                elif task == "k1":
                    pe.wait_ge(qk1_out.sem, qk1_out.after(n, 1))
                    project(ms[:], W["wk1"], xT_s, slice(0, MEM)).then_inc(proj1.sem, 1)
                elif task == "v1":
                    pe.wait_ge(qk1_out.sem, qk1_out.after(n, 2))
                    project_rows(ms, MEM, xT_s, W["wv1"], slice(0, MEM), range(TB)).then_inc(proj1.sem, 1)
                elif task in ("s0", "s1", "s23"):
                    if task == "s0":
                        pe.wait_ge(v1_out.sem, v1_out.after(n, 1))
                    else:
                        pe.wait_ge(a1_out.sem, a1_out.after(n, int(task[1])))
                    at = 0
                    for i in map(int, task[1:]):
                        last = mm(ms[:, at:at + T - i * P], k1T[:, i * P:i * P + P], q1T[:, i * P:T], True, True)
                        at += T - i * P
                    last.then_inc(lin_s.sem, 1)
                elif task == "o1":
                    pe.wait_ge(a1_out.sem, a1_out.after(n, 3))
                    for i in range(TB):
                        last = mm(ms[:, i * P:T], v1[:, i, :], a1[:, A_AT[i]:A_AT[i] + T - i * P], i == 0, i == TB - 1)
                    last.then_inc(lin_o.sem, 1)
                elif task in ("y01", "y23"):
                    if task == "y01":
                        pe.wait_ge(o1_out.sem, o1_out.after(n, 1))
                    else:
                        pe.wait_ge(res_out[0].sem, res_out[0].after(n, 1))
                    for j, t in enumerate(map(int, task[1:])):
                        last = mm(ms[:, j * D:j * D + D], o1T[:, t * P:t * P + P], W["wo1"][:], True, True)
                    last.then_inc(lin_y.sem, 1)
                elif task in ("x0", "x1"):
                    c = int(task[1])
                    if c == 0:
                        pe.wait_ge(ln_out[0].sem, ln_out[0].after(n, TB))
                    else:
                        pe.wait_ge(x1t_out.sem, x1t_out.after(n, 1))
                    transpose_rows(ms, x1, c).then_inc(x1t.sem, 1)
                elif task in ("kc0", "kc1"):
                    c = int(task[2])
                    project(ms[:], W["wk2"], ctxT_s, slice(c * P, c * P + P)).then_inc(projc.sem, 1)
                elif task in ("qc0", "qc1"):
                    c = int(task[2])
                    pe.wait_ge(kc_out.sem, kc_out.after(n, 2 * c + 2))
                    project(ms[:], W["wq2"], x1T, slice(c * P, c * P + P)).then_inc(projq.sem, 1)

            def cross_v(n, half):
                pe.wait_ge(ctx_in.sem, ctx_in.after(n, 1))
                project_rows(V2_BANK[half], D, ctxT_s, W["wv2"], slice(0, D), (2 * half, 2 * half + 1)) \
                    .then_inc(projc.sem, 1)

            def ring_tile(b, tile, more, e=None):
                kind, elt, layer, n = tile
                at = ring_at(tile, more)
                e = b + elt if e is None else e
                bank = mx[:, at % 2, :]
                if more is not None or at >= 2:
                    pe.wait_ge(ring_out.sem, ring_out.after(b, at - 1))
                if kind == "max":
                    h, t = n // TB, n % TB
                    if n % (MAXES // DC) == 0:
                        c = n // (MAXES // DC)
                        pe.wait_ge(stack_in[c].sem, stack_in[c].after(e, (layer + 1) * 2 * TERMS))
                    last = mm(bank, qs[0:ROWS, h, t * P:t * P + P], ks[0:ROWS, h, :], True, True)
                elif kind == "shift":
                    pe.wait_ge(shift_cut.sem, shift_cut.after(e, (layer * G + n + 1) * SHIFT))
                    last = nc.tensor.transpose(bank[0:SHIFT * HG * TB, 0:P // 2].bitcast(BF16), shift_n[:, n, :], identb[:])
                else:
                    pe.wait_ge(oT_out.sem, oT_out.after(e, layer * G + n + 1))
                    for t in range(TB):
                        last = nc.tensor.transpose(bank[:, t * P:t * P + P], oT[:, t * P:t * P + P], ident[:])
                last.then_inc(ring.sem, 1)

            def scores(b, layer, s, pair):
                g, kb = s // TB, s % TB
                if s >= 1:
                    pe.wait_ge(exp_out.sem, exp_out.after(b, (layer * STEPS + s - 1) * 2 + pair + 1))
                if kb == 0 and pair == 0:
                    pe.wait_ge(shift_in.sem, shift_in.after(b, layer * G + g + 1))
                for j in range(2):
                    h = HG * g + 2 * pair + j
                    last = mm(sc[:, 2 * pair + j, :], ks[0:ROWS + SHIFT, h, kb * P:kb * P + P],
                              qs[0:ROWS + SHIFT, h, :], True, True)
                last.then_inc(score.sem, 1)

            def values(b, layer, s):
                g, kb = s // TB, s % TB
                pe.wait_ge(exp_out.sem, exp_out.after(b, (layer * STEPS + s + 1) * 2))
                if kb == 0:
                    pe.wait_ge(oT_out.sem, oT_out.after(b, layer * G + g))
                for j in range(HG):
                    last = mm(op[32 * j:32 * j + 32, :], v2[layer][:, kb, HG * g + j, :], probs[:, s % 2, j, :],
                              kb == 0, kb == TB - 1)
                last.then_inc(pv.sem, 1)

            def mixture(b, n):
                t, pair = n // (E // 2), n % (E // 2)
                bank = ms[:] if MOE_BANK[n] == 4 else op[:] if MOE_BANK[n] == 5 else sc[:, MOE_BANK[n], :]
                before = [m for m in range(n) if MOE_BANK[m] == MOE_BANK[n]]
                if before:
                    pe.wait_ge(moe_out.sem, moe_out.after(b, 2 * (before[-1] + 1)))
                elif MOE_BANK[n] == 4:
                    pe.wait_ge(moe_b_out.sem, moe_b_out.after(b, 2))
                elif MOE_BANK[n] in (1, 2):
                    pe.wait_ge(v3_out.sem, v3_out.after(b, MOE_BANK[n]))
                else:
                    pe.wait_ge(qk3_out.sem, qk3_out.after(b, {3: 4, 5: 6, 0: 8}[MOE_BANK[n]]))
                for k, (i, j) in enumerate(((0, 0), (1, 0), (0, 1))):
                    for c in range(DC):
                        last = mm(bank, x2T_part[i][:, c, t * P:t * P + P].bitcast(F32R),
                                  we_part[j][:, c, 2 * pair * D:2 * pair * D + 2 * D].bitcast(F32R),
                                  k == 0 and c == 0, k == 2 and c == DC - 1)
                last.then_inc(moe_t.sem, 1)

            def steps(b, layer, more):
                for s in range(STEPS):
                    front, spread, behind = step_tiles(layer, s, more)
                    for tile in front:
                        ring_tile(b, tile, more)
                    for k in range(4):
                        if k < len(spread):
                            ring_tile(b, spread[k], more)
                        if k < 2:
                            scores(b, layer, s, k)
                        elif k == 2 and s >= 1:
                            if s == 1 and layer == 0:
                                pe.wait_ge(vc_out.sem, vc_out.after(b, 2))
                            values(b, layer, s - 1)
                    for tile in spread[4:] + behind:
                        ring_tile(b, tile, more)
                    task = beside(layer, s, more)
                    if isinstance(task, int):
                        if more and task == 12:
                            pe.wait_ge(qc_out.sem, qc_out.after(b + 1, 2))
                        if more and task == 13:
                            pe.wait_ge(qc_out.sem, qc_out.after(b + 1, 4))
                        mixture(b, task)
                    elif task:
                        if task == "q1":
                            pe.wait_ge(moe_out.sem, moe_out.after(b, 0))
                        if task in ("kc0", "kc1"):
                            pe.wait_ge(moe_out.sem, moe_out.after(b, 2 * {"kc0": 12, "kc1": 13}[task]))
                        spare(task, b + 1)
                spread, behind = tail_tiles(layer, more)
                for tile in spread[:2]:
                    ring_tile(b, tile, more)
                values(b, layer, STEPS - 1)
                for tile in spread[2:] + behind:
                    ring_tile(b, tile, more)

            def turn(b, more):
                pe.wait_ge(exp_out.sem, exp_out.after(b, 0))
                steps(b, 0, more)
                pe.wait_ge(exp_out.sem, exp_out.after(b, STEPS * 2))
                pe.wait_ge(ring_out.sem, ring_out.after(b, ring_at(("heads", 0, 0, G - 1), more) + 1))
                for c in range(DC):
                    transpose_rows(sc[:, c, :], heads, c).then_inc(ht.sem, 1)
                pe.wait_ge(ht_out.sem, ht_out.after(b, DC))
                for h in range(2):
                    project_rows(sc[:, 2 + h, :], D, headsT, W["wo2"], slice(0, D), (2 * h, 2 * h + 1)).then_inc(cross_y.sem, 1)
                if more:
                    pe.wait_ge(x1t_out.sem, x1t_out.after(b + 1, DC))
                    cross_v(b + 1, 0)
                    pe.wait_ge(oT_out.sem, oT_out.after(b, G))
                    cross_v(b + 1, 1)
                for t in range(TB):
                    pe.wait_ge(ln_out[1].sem, ln_out[1].after(b, t + 1))
                    for c in range(DC):
                        last = nc.tensor.transpose(sc[:, c, t * P:(t + 1) * P], x2[:, t, c * P:(c + 1) * P], ident[:])
                last.then_inc(x2t.sem, 1)
                pe.wait_ge(x2t_out.sem, x2t_out.after(b, DC))
                if more:
                    pe.wait_ge(vc_out.sem, vc_out.after(b + 1, 2))
                else:
                    pe.wait_ge(oT_out.sem, oT_out.after(b, G))
                w3 = W["wqkv3"]
                for n, bank in enumerate(QK3_BANK):
                    c, k = n // 2, 1 - n % 2
                    project(bank, w3, x2T, slice(k * D + c * P, k * D + c * P + P)).then_inc(proj3.sem, 1)
                    if n == 1:
                        project_rows(ms, E, x2T, W["wg"], slice(0, E), range(TB)).then_inc(gate.sem, 1)
                pe.wait_ge(qk3_out.sem, qk3_out.after(b, 2))
                for h in range(2):
                    project_rows(sc[:, 1 + h, :], D, x2T, w3, slice(2 * D, 3 * D), (2 * h, 2 * h + 1)).then_inc(proj3v.sem, 1)
                pe.wait_ge(x_cut.sem, x_cut.after(b, 3))
                for n in range(MOE_LEAD):
                    mixture(b, n)
                tiles = first_tiles(0, 1)
                ring_tile(b, tiles[0], more)
                pe.wait_ge(g_step.sem, g_step.after(b, 12))
                for t in range(TB):
                    last = nc.tensor.transpose(ms[:, t * P:t * P + P], comb[:, t, :], ident[:])
                last.then_inc(cT.sem, 1)
                for tile in tiles[1:3]:
                    ring_tile(b, tile, more)
                pe.wait_ge(cT_out.sem, cT_out.after(b, 1))
                for h in range(2):
                    if h == 1:
                        pe.wait_ge(moe_b_out.sem, moe_b_out.after(b, 1))
                    for j in range(2):
                        t = 2 * h + j
                        last = mm(ms[:, j * D:j * D + D], combT[:, t * P:t * P + P], W["be"][:], True, True)
                    last.then_inc(moe_b.sem, 1)
                    if h == 0:
                        for tile in tiles[3:5]:
                            ring_tile(b, tile, more)
                done = MOE_LEAD
                for n, tile in enumerate(tiles[5:]):
                    ring_tile(b, tile, more)
                    if n % 2 == 0 and done < MOE_EARLY:
                        mixture(b, done)
                        done += 1
                while done < MOE_EARLY:
                    mixture(b, done)
                    done += 1
                pe.wait_ge(moe_out.sem, moe_out.after(b, 2 * MOE_EARLY))
                steps(b, 1, more)

            for signal in (score, pv):
                signal.prime(pe)
            pe.wait_ge(w_in.sem, 16 * len(EARLY))
            for task in BESIDE[0].values():
                spare(task, 0)
            pe.wait_ge(w_late.sem, 16 * len(LATE))
            pe.wait_ge(const.sem, 3)
            pe.wait_ge(fills.sem, 4)
            pe.wait_ge(x1t_out.sem, x1t_out.after(0, DC))
            for half in range(2):
                cross_v(0, half)
            pe.wait_ge(vc_out.sem, vc_out.after(0, 1))
            for task in BESIDE[1].values():
                if task == "kc1":
                    pe.wait_ge(qc_out.sem, qc_out.after(0, 2))
                if not isinstance(task, int):
                    spare(task, 0)
            for tile in first_tiles(1, 0):
                ring_tile(0, tile, None, e=0)
            pe.wait_ge(w_cut.sem, 3)
            with pe.Fori(0, B - 1) as b:
                turn(b, True)
            turn(B - 1, False)

        @block.scalar
        def _(act):
            def copy(dst, src, bias=None, scale=1.0):
                if bias is None:
                    return nc.scalar.activation(dst, src, ACT.Copy)
                return nc.scalar.activation(dst, src, ACT.Identity, bias=bias, scale=scale)

            def cut(name, c, bank, bias, scale, done):
                copy(part_f[name][:, c, :], bank, bias[:, c:c + 1], scale).then_inc(done.sem, 1)
                copy(part[name][:, c, 0, :], bank, bias[:, c:c + 1], scale).then_inc(done.sem, 1)

            def spare(task, n):
                if task in ("q1", "k1"):
                    act.wait_ge(proj1.sem, proj1.after(n, 1 + (task == "k1")))
                    dst, bias = (q1T, "bq1") if task == "q1" else (k1T, "bk1")
                    copy(dst[:], ms[:], W[bias][:, 0:1]).then_inc(qk1_out.sem, 1)
                elif task == "o1":
                    act.wait_ge(lin_o.sem, lin_o.after(n, 1))
                    copy(o1T[:], ms[:]).then_inc(o1_out.sem, 1)
                elif task in ("x0", "x1"):
                    c = int(task[1])
                    act.wait_ge(x1t.sem, x1t.after(n, c + 1))
                    copy(x1T[:, c, :], ms[:]).then_inc(x1t_out.sem, 1)
                elif task in ("kc0", "kc1", "qc0", "qc1"):
                    c = int(task[2])
                    act.wait_ge(stack_in[c].sem, stack_in[c].after(n, 0))
                    if task[0] == "k":
                        act.wait_ge(projc.sem, projc.after(n, 2 + c + 1))
                        cut("k", c, ms[:], W["bk2"], 1.0, kc_out)
                    else:
                        act.wait_ge(projq.sem, projq.after(n, c + 1))
                        cut("q", c, ms[:], bq2, HD ** -0.5, qc_out)

            def exps(b, layer, s, pair):
                act.wait_ge(score.sem, score.after(b, (layer * STEPS + s) * 2 + pair + 1))
                if pair == 0:
                    act.wait_ge(pv.sem, pv.after(b, layer * STEPS + max(s - 1, 0)))
                nc.scalar.activation(probs[:, s % 2, 2 * pair:2 * pair + 2, :], sc[:, 2 * pair:2 * pair + 2, :],
                                     ACT.Exp).then_inc(exp_out.sem, 1)

            def group_out(b, layer, g, more):
                act.wait_ge(pv.sem, pv.after(b, layer * STEPS + TB * g + TB))
                if g >= 1:
                    act.wait_ge(ring.sem, ring.after(b, ring_at(("heads", 0, layer, g - 1), more) + 1))
                copy(oT[:], op[:]).then_inc(oT_out.sem, 1)

            def mixture(b, n):
                t, pair = n // (E // 2), n % (E // 2)
                bank = ms[:] if MOE_BANK[n] == 4 else op[:] if MOE_BANK[n] == 5 else sc[:, MOE_BANK[n], :]
                act.wait_ge(moe_t.sem, moe_t.after(b, n + 1))
                act.wait_ge(acc.sem, acc.after(b, 2 + 2 * max(n - 3, 0)))
                for j in range(2):
                    e = 2 * pair + j
                    nc.scalar.activation(moe[:, n % 4, j * D:j * D + D], bank[:, j * D:j * D + D], ACT.Copy,
                                         scale=comb[:, t, e:e + 1]).then_inc(moe_out.sem, 1)

            def steps(b, layer, more):
                for s in range(STEPS + 1):
                    if s < STEPS:
                        exps(b, layer, s, 0)
                    task = beside(layer, s - 1, more)
                    if isinstance(task, int):
                        mixture(b, task)
                    elif task:
                        spare(task, b + 1)
                    if s < STEPS:
                        exps(b, layer, s, 1)
                    if s % TB == 0 and s >= 1:
                        group_out(b, layer, s // TB - 1, more)

            def turn(b, more):
                steps(b, 0, more)
                act.wait_ge(ht.sem, ht.after(b, 1))
                copy(headsT[:, 0, :], sc[:, 0, :]).then_inc(ht_out.sem, 1)
                act.wait_ge(x2t.sem, x2t.after(b, 1))
                copy(x2T[:, 0, :], sc[:, 0, :]).then_inc(x2t_out.sem, 1)
                for n, bank in enumerate(QK3_BANK):
                    c = n // 2
                    act.wait_ge(stack_in[c].sem, stack_in[c].after(b, 2 * TERMS))
                    act.wait_ge(proj3.sem, proj3.after(b, n + 1))
                    if n % 2 == 1:
                        cut("q", c, bank, bq3, HD ** -0.5, qk3_out)
                    else:
                        cut("k", c, bank, W["bk3"], 1.0, qk3_out)
                    if n == 1:
                        act.wait_ge(g_step.sem, g_step.after(b, 3))
                        nc.scalar.activation(g_e[:], g_l[:], ACT.Exp).then_inc(g_exp.sem, 1)
                act.wait_ge(cT.sem, cT.after(b, 1))
                copy(combT[:], ms[:]).then_inc(cT_out.sem, 1)
                for h in range(2):
                    act.wait_ge(moe_b.sem, moe_b.after(b, h + 1))
                    act.wait_ge(acc.sem, acc.after(b, 0))
                    copy(moe[:, h, :], ms[:]).then_inc(moe_b_out.sem, 1)
                for n in range(MOE_EARLY):
                    mixture(b, n)
                steps(b, 1, more)

            for signal in (exp_out, moe_out, oT_out):
                signal.prime(act)
            for name in EARLY:
                if name not in ("wq1", "wk1", "ident"):
                    act.dma_start(W[name][:], w[name]).then_inc(w_in.sem, 16)
            act.wait_ge(w_in.sem, 16 * len(EARLY))
            nc.scalar.copy(identb[:], ident[:]).then_inc(const.sem, 1)
            for task in BESIDE[0].values():
                spare(task, 0)
            act.wait_ge(w_late.sem, 16 * len(LATE))
            nc.scalar.mul(bq2[:], W["bq2"][:], HD ** -0.5).then_inc(const.sem, 1)
            nc.scalar.mul(bq3[:], W["bq3"][:], HD ** -0.5).then_inc(const.sem, 1)
            act.wait_ge(const.sem, 3)
            for task in BESIDE[1].values():
                if not isinstance(task, int):
                    spare(task, 0)
            with act.Fori(0, B - 1) as b:
                turn(b, True)
            turn(B - 1, False)

        @block.vector
        def _(dve):
            def spare(task, n):
                if task == "v1":
                    dve.wait_ge(proj1.sem, proj1.after(n, 3))
                    nc.vector.tensor_tensor(v1[:], ms[:].rearrange("p (n m) -> p n m", n=TB),
                                            W["bv1"][:].rearrange("p (o m) -> p o m", o=1).broadcast_to([P, TB, MEM]),
                                            ALU.add).then_inc(v1_out.sem, 1)
                elif task in ("s0", "s1", "s23"):
                    dve.wait_ge(lin_s.sem, lin_s.after(n, ("s0", "s1", "s23").index(task) + 1))
                    at = 0
                    for i in map(int, task[1:]):
                        wide = T - i * P
                        last = nc.vector.tensor_tensor(a1[:, A_AT[i]:A_AT[i] + wide], ms[:, at:at + wide],
                                                       W["decay"][:, 0:wide], ALU.mult)
                        at += wide
                    last.then_inc(a1_out.sem, 1)
                elif task in ("y01", "y23"):
                    h = int(task == "y23")
                    dve.wait_ge(xb_out.sem, xb_out.after(n, 1))
                    dve.wait_ge(lin_y.sem, lin_y.after(n, h + 1))
                    nc.vector.tensor_tensor(res[:, 2 * h:2 * h + 2, :], ms[:].rearrange("p (n d) -> p n d", n=2),
                                            x_s[:, 2 * h:2 * h + 2, :], ALU.add).then_inc(res_out[0].sem, 1)
                elif task in ("qc0", "qc1"):
                    cut(n, 0, int(task[2]), qc_out)

            def values_in(n, dst, bank, h, bias, signal, done):
                dve.wait_ge(signal.sem, signal.after(n, done))
                return nc.vector.tensor_tensor(
                    dst[:, 2 * h:2 * h + 2, :, 0:HD], bank.rearrange("p (n h d) -> p n h d", n=2, h=H),
                    bias[:].rearrange("p (o h d) -> p o h d", o=1, h=H).broadcast_to([P, 2, H, HD]), ALU.add)

            def cross_v(n):
                for h in range(2):
                    values_in(n, v2[0], V2_BANK[h], h, W["bv2"], projc, h + 1).then_inc(vc_out.sem, 1)

            def high(dst, rest, src, signal, at):
                nc.vector.scalar_tensor_tensor(out=rest[:], in0=src[:], scalar=SPLIT, in1=src[:],
                                               op0=ALU.mult, op1=ALU.subtract).then_inc(signal.sem, 1)
                dve.wait_ge(signal.sem, at)
                nc.vector.scalar_tensor_tensor(out=dst[:].bitcast(F32R), in0=src[:], scalar=SPLIT, in1=rest[:],
                                               op0=ALU.mult, op1=ALU.subtract).then_inc(signal.sem, 1)

            def layer_norm(k, n, dst, residual=None):
                step = ln_step[k]
                for t in range(TB):
                    if residual and t % 2 == 0:
                        residual(t // 2)
                    dve.wait_ge(res_out[k].sem, res_out[k].after(n, t // 2 + 1))
                    nc.vector.bn_stats(stats[:, t, :], res[:, t, :]).then_inc(step.sem, 1)
                for t in range(TB):
                    dve.wait_ge(step.sem, step.after(n, t + 1))
                    stand(dve, "dve")
                    nc.vector.bn_aggr(mv[:, t, :], stats[:, t, :]).then_inc(step.sem, 1)
                dve.wait_ge(step.sem, step.after(n, 8))
                nc.vector.tensor_scalar(var[:], mv[:, :, 1], EPS, None, ALU.add).then_inc(step.sem, 1)
                dve.wait_ge(step.sem, step.after(n, 9))
                nc.vector.tensor_scalar(seed[:], var[:].bitcast(I32), 1, None, ALU.logical_shift_right) \
                    .then_inc(step.sem, 1)
                dve.wait_ge(step.sem, step.after(n, 10))
                nc.vector.tensor_scalar(rstd_i[:], seed[:], -1.0, float(0x5F3759DF), ALU.mult, ALU.add) \
                    .then_inc(step.sem, 1)
                guess = rstd_i[:].bitcast(F32)
                for i in range(3):
                    m = 11 + 3 * i
                    dve.wait_ge(step.sem, step.after(n, m))
                    nc.vector.scalar_tensor_tensor(out=newton[:, 0, :], in0=guess, scalar=-0.5, in1=guess,
                                                   op0=ALU.mult, op1=ALU.mult).then_inc(step.sem, 1)
                    dve.wait_ge(step.sem, step.after(n, m + 1))
                    nc.vector.tensor_tensor(newton[:, 1, :], newton[:, 0, :], var[:], ALU.mult).then_inc(step.sem, 1)
                    dve.wait_ge(step.sem, step.after(n, m + 2))
                    nc.vector.scalar_tensor_tensor(out=rstd[:, i, :], in0=newton[:, 1, :], scalar=1.5, in1=guess,
                                                   op0=ALU.add, op1=ALU.mult).then_inc(step.sem, 1)
                    guess = rstd[:, i, :]
                dve.wait_ge(step.sem, step.after(n, 20))
                for t in range(TB):
                    nc.vector.tensor_scalar(dst[:, t, :], res[:, t, :], mv[:, t, 0:1], rstd[:, 2, t:t + 1],
                                            ALU.subtract, ALU.mult).then_inc(ln_out[k].sem, 1)

            def cut(n, layer, c, done):
                m = (layer * DC + c) * 3
                dve.wait_ge(done.sem, done.after(n, 2 * c + 2 if layer == 0 else 4 * c + 4))
                if m:
                    dve.wait_ge(q_step.sem, q_step.after(n, m))
                nc.vector.tensor_tensor(part_r["q"][:], part_f["q"][:, c, :], part["q"][:, c, 0, :], ALU.subtract) \
                    .then_inc(q_step.sem, 1)
                dve.wait_ge(q_step.sem, q_step.after(n, m + 1))
                nc.vector.tensor_copy(part["q"][:, c, 1, :], part_r["q"][:]).then_inc(q_step.sem, 1)
                dve.wait_ge(q_step.sem, q_step.after(n, m + 2))
                nc.vector.tensor_tensor(part["q"][:, c, 2, :], part_r["q"][:], part["q"][:, c, 1, :], ALU.subtract) \
                    .then_inc(q_step.sem, 1)

            def ring_tile(b, tile, more, e=None):
                kind, elt, layer, n = tile
                at = ring_at(tile, more)
                e = b + elt if e is None else e
                bank = mx[:, at % 2, :]
                dve.wait_ge(ring.sem, ring.after(b, at + 1))
                if kind == "max":
                    nc.vector.tensor_reduce(maxes[:, n:n + 1], bank, AX_X, ALU.max).then_inc(ring_out.sem, 1)
                    g, size = n // (HG * TB), HG * TB
                    if n % size == size - 1:
                        m = maxes[:, g * size:(g + 1) * size]
                        dve.wait_ge(ring_out.sem, ring_out.after(b, at + 1))
                        nc.vector.tensor_scalar(shift_n[:, g, 0:size], m, -1.0, None, ALU.mult).then_inc(shift_cut.sem, 1)
                        dve.wait_ge(shift_cut.sem, shift_cut.after(e, (layer * G + g) * SHIFT + 1))
                        nc.vector.scalar_tensor_tensor(out=shift_n[:, g, size:2 * size], in0=m, scalar=-1.0,
                                                       in1=shift_n[:, g, 0:size], op0=ALU.mult,
                                                       op1=ALU.subtract).then_inc(shift_cut.sem, 1)
                elif kind == "shift":
                    nc.vector.tensor_copy(shift_r[:, n, :], bank[0:SHIFT * HG * TB, 0:P // 2].bitcast(BF16)) \
                        .then_inc(ring_out.sem, 1)
                else:
                    v = bank.rearrange("p (n h d) -> p n h d", n=TB, h=HG)
                    nc.vector.reciprocal(rsum[:, n % 2], v[:, :, :, HD]).then_inc(rs.sem, 1)
                    dve.wait_ge(rs.sem, rs.after(b, layer * G + n + 1))
                    dst = heads[:, :, n * HG * HD:(n + 1) * HG * HD].rearrange("p n (h d) -> p n h d", h=HG)
                    nc.vector.tensor_tensor(dst, v[:, :, :, 0:HD],
                                            rsum[:, n % 2].rearrange("p n (h o) -> p n h o", o=1).broadcast_to([P, TB, HG, HD]),
                                            ALU.mult).then_inc(ring_out.sem, 1)

            def steps(b, layer, more):
                for s in range(STEPS):
                    for tiles in step_tiles(layer, s, more):
                        for tile in tiles:
                            ring_tile(b, tile, more)
                    for at in (s - 1, s):
                        task = beside(layer, at, more)
                        if isinstance(task, str) and (task in ("qc0", "qc1")) == (at == s - 1):
                            spare(task, b + 1)
                    if more and layer == 0 and s == NORM_AT:
                        dve.wait_ge(x1b_out.sem, x1b_out.after(b, 1))
                        layer_norm(0, b + 1, x1)
                for tiles in tail_tiles(layer, more):
                    for tile in tiles:
                        ring_tile(b, tile, more)

            def g_wait(b, n):
                dve.wait_ge(g_step.sem, g_step.after(b, n))

            def combine(b):
                dve.wait_ge(gate.sem, gate.after(b, 1))
                wide = [P, TB, E]
                nc.vector.tensor_tensor(g_p[:], ms[:, 0:TB * E].rearrange("p (n e) -> p n e", n=TB),
                                        W["bg"][:].rearrange("p (o e) -> p o e", o=1).broadcast_to(wide),
                                        ALU.add).then_inc(g_step.sem, 1)
                g_wait(b, 1)
                nc.vector.tensor_reduce(g_m[:], g_p[:], AX_X, ALU.max).then_inc(g_step.sem, 1)
                g_wait(b, 2)
                nc.vector.tensor_tensor(g_l[:], g_p[:], g_m[:].rearrange("p (n o) -> p n o", o=1).broadcast_to(wide),
                                        ALU.subtract).then_inc(g_step.sem, 1)
                dve.wait_ge(g_exp.sem, g_exp.after(b, 1))
                nc.vector.tensor_reduce(g_s[:, 0, :], g_e[:], AX_X, ALU.add).then_inc(g_step.sem, 1)
                g_wait(b, 4)
                nc.vector.reciprocal(g_s[:, 1, :], g_s[:, 0, :]).then_inc(g_step.sem, 1)
                g_wait(b, 5)
                nc.vector.tensor_tensor(g_p[:], g_e[:],
                                        g_s[:, 1, :].rearrange("p (n o) -> p n o", o=1).broadcast_to(wide),
                                        ALU.mult).then_inc(g_step.sem, 1)
                g_wait(b, 6)
                mine = g_p[:].rearrange("p n (e o) -> p n e o", o=1).broadcast_to([P, TB, E, E])
                other = g_p[:].rearrange("p n (o e) -> p n o e", o=1).broadcast_to([P, TB, E, E])
                nc.vector.tensor_tensor(above[:], other, mine, ALU.is_gt).then_inc(g_step.sem, 1)
                nc.vector.tensor_tensor(tied[:], other, mine, ALU.is_equal).then_inc(g_step.sem, 1)
                g_wait(b, 8)
                earlier = W["earlier"][:].rearrange("p (o m) -> p o m", o=1).broadcast_to([P, TB, E * E])
                nc.vector.tensor_tensor(tied[:].rearrange("p n e m -> p n (e m)"),
                                        tied[:].rearrange("p n e m -> p n (e m)"), earlier, ALU.mult) \
                    .then_inc(g_step.sem, 1)
                g_wait(b, 9)
                nc.vector.tensor_tensor(above[:], above[:], tied[:], ALU.add).then_inc(g_step.sem, 1)
                g_wait(b, 10)
                nc.vector.tensor_reduce(rank[:], above[:], AX_X, ALU.add).then_inc(g_step.sem, 1)
                g_wait(b, 11)
                nc.vector.scalar_tensor_tensor(out=comb[:, :, 0:E], in0=rank[:], scalar=2.0, in1=g_p[:],
                                               op0=ALU.is_lt, op1=ALU.mult).then_inc(g_step.sem, 1)

            def turn(b, more):
                steps(b, 0, more)
                dve.wait_ge(ht.sem, ht.after(b, 2))
                nc.vector.tensor_copy(headsT[:, 1, :], sc[:, 1, :]).then_inc(ht_out.sem, 1)
                dve.wait_ge(x1b_out.sem, x1b_out.after(b, 1))
                if more:
                    dve.wait_ge(ln_out[0].sem, ln_out[0].after(b + 1, TB))

                def cross_sum(h):
                    dve.wait_ge(cross_y.sem, cross_y.after(b, h + 1))
                    nc.vector.tensor_tensor(res[:, 2 * h:2 * h + 2, :], sc[:, 2 + h, :].rearrange("p (n d) -> p n d", n=2),
                                            x1b[:, 2 * h:2 * h + 2, :], ALU.add).then_inc(res_out[1].sem, 1)

                layer_norm(1, b, x2, cross_sum)
                dve.wait_ge(x2t.sem, x2t.after(b, 1))
                nc.vector.tensor_copy(x2T[:, 1, :], sc[:, 1, :]).then_inc(x2t_out.sem, 1)
                if more:
                    cross_v(b + 1)
                dve.wait_ge(x2t_out.sem, x2t_out.after(b, DC))
                high(x2T_part[0], x_rest, x2T, x_cut, x_cut.after(b, 1))
                cut(b, 1, 0, qk3_out)
                combine(b)
                for h in range(2):
                    values_in(b, v2[1], sc[:, 1 + h, :], h, W["bv3"], proj3v, h + 1).then_inc(v3_out.sem, 1)
                cut(b, 1, 1, qk3_out)
                for tile in first_tiles(0, 1):
                    ring_tile(b, tile, more)
                steps(b, 1, more)
                dve.wait_ge(acc.sem, acc.after(b, 2 + 2 * MOE_TILES))
                dve.wait_ge(ring_out.sem, ring_out.after(b, ring_at(("heads", 0, 1, G - 1), more) + 1))
                for h in range(2):
                    nc.vector.tensor_tensor(res[:, 2 * h:2 * h + 2, :], heads[:, 2 * h:2 * h + 2, :],
                                            x2[:, 2 * h:2 * h + 2, :], ALU.add).then_inc(res_out[2].sem, 1)
                dve.wait_ge(y_free.sem, y_free.after(b, 0))
                layer_norm(2, b, y)

            for n in range(LAYERS):
                nc.vector.memset(v2[n][:, :, :, HD:32], 1.0).then_inc(fills.sem, 1)
            nc.vector.memset(ks[ROWS:P, :, :], 1.0).then_inc(fills.sem, 1)
            nc.vector.memset(comb[:], 0.0).then_inc(fills.sem, 1)
            dve.wait_ge(w_in.sem, 16 * len(EARLY))
            for task in BESIDE[0].values():
                spare(task, 0)
                if task == "y23":
                    layer_norm(0, 0, x1)
            dve.wait_ge(w_late.sem, 16 * len(LATE))
            high(we_part[0], w_rest, we_all, w_cut, 1)
            dve.wait_ge(fills.sem, 4)
            cross_v(0)
            for task in BESIDE[1].values():
                if not isinstance(task, int):
                    spare(task, 0)
            for tile in first_tiles(1, 0):
                ring_tile(0, tile, None, e=0)
            with dve.Fori(0, B - 1) as b:
                turn(b, True)
            turn(B - 1, False)

        @block.gpsimd
        def _(pool):
            def input_bias(n):
                pool.wait_ge(x_in.sem, x_in.after(n, 1))
                nc.gpsimd.tensor_tensor(x_s[:], x_s[:],
                                        W["bo1"][:].rearrange("p (o d) -> p o d", o=1).broadcast_to([P, TB, D]),
                                        ALU.add).then_inc(xb_out.sem, 1)

            def cut(n, layer, c, done, at):
                m = (layer * DC + c) * 3
                pool.wait_ge(done.sem, done.after(n, at))
                if m:
                    pool.wait_ge(k_step.sem, k_step.after(n, m))
                nc.gpsimd.tensor_tensor(part_r["k"][:], part_f["k"][:, c, :], part["k"][:, c, 0, :], ALU.subtract) \
                    .then_inc(k_step.sem, 1)
                pool.wait_ge(k_step.sem, k_step.after(n, m + 1))
                stand(pool, "pool")
                nc.gpsimd.tensor_copy(part["k"][:, c, 1, :], part_r["k"][:]).then_inc(k_step.sem, 1)
                pool.wait_ge(k_step.sem, k_step.after(n, m + 2))
                nc.gpsimd.tensor_tensor(part["k"][:, c, 2, :], part_r["k"][:], part["k"][:, c, 1, :], ALU.subtract) \
                    .then_inc(k_step.sem, 1)

            def turn(b, more):
                pool.wait_ge(ln_out[0].sem, ln_out[0].after(b, TB))
                nc.gpsimd.tensor_tensor(x1b[:], x1[:],
                                        W["bo2"][:].rearrange("p (o d) -> p o d", o=1).broadcast_to([P, TB, D]),
                                        ALU.add).then_inc(x1b_out.sem, 1)
                if more:
                    input_bias(b + 1)
                pool.wait_ge(x_cut.sem, x_cut.after(b, 2))
                nc.gpsimd.tensor_tensor(x2T_part[1][:].bitcast(F32R), x2T[:], x2T_part[0][:], ALU.subtract).then_inc(x_cut.sem, 1)
                for c in range(DC):
                    cut(b, 1, c, qk3_out, 4 * c + 2)
                for h in range(2):
                    pool.wait_ge(moe_b_out.sem, moe_b_out.after(b, h + 1))
                    nc.gpsimd.tensor_tensor(x2[:, 2 * h:2 * h + 2, :], x2[:, 2 * h:2 * h + 2, :],
                                            moe[:, h, :].rearrange("p (n d) -> p n d", n=2), ALU.add).then_inc(acc.sem, 1)
                for n in range(MOE_TILES):
                    t = n // (E // 2)
                    for j in range(2):
                        pool.wait_ge(moe_out.sem, moe_out.after(b, 2 * n + j + 1))
                        pool.wait_ge(acc.sem, acc.after(b, 2 + 2 * n + j))
                        nc.gpsimd.tensor_tensor(x2[:, t, :], x2[:, t, :], moe[:, n % 4, j * D:j * D + D], ALU.add) \
                            .then_inc(acc.sem, 1)
                    if more and n in (MOE_EARLY - 1, MOE_EARLY):
                        c = n - (MOE_EARLY - 1)
                        cut(b + 1, 0, c, kc_out, 2 * c + 2)
                pool.wait_ge(ln_out[2].sem, ln_out[2].after(b, TB))
                stand(pool, "pool")
                nc.gpsimd.dma_start(out[bass.ds(b, 1)].rearrange("o (n p) d -> p (o n) d", p=P), y[:]) \
                    .then_inc(y_out.sem, 16)
                pool.wait_ge(y_out.sem, y_out.after(b, 1))
                pool.sem_inc(y_free.sem, 1)

            y_free.prime(pool)
            acc.prime(pool)
            pool.wait_ge(w_in.sem, 16 * len(EARLY))
            input_bias(0)
            for c in range(DC):
                cut(0, 0, c, kc_out, 2 * c + 2)
            pool.wait_ge(w_late.sem, 16 * len(LATE))
            pool.wait_ge(w_cut.sem, 2)
            nc.gpsimd.tensor_tensor(we_part[1][:].bitcast(F32R), we_all[:], we_part[0][:], ALU.subtract).then_inc(w_cut.sem, 1)
            with pool.Fori(0, B - 1) as b:
                turn(b, True)
            turn(B - 1, False)


def by_chunk(a):
    return a.reshape(DC, P, -1).transpose(1, 0, 2)


def head_rows(a):
    return a.reshape(DC, H // DC, HD, -1).transpose(0, 2, 1, 3).reshape(D, -1)


def kernel(**inputs):
    import numpy as np
    import concourse.bacc as bacc
    from concourse.bass_utils import run_bass_kernel_spmd as run

    def arr(name):
        return np.asarray(inputs[name])

    def rows(a):
        return np.broadcast_to(a.reshape(1, -1), (P, a.size))

    x, ctx = arr("x"), arr("ctx_1024")
    attn, cross, ffn = "L0_attn_", "L0_xattn_", "L0_ffn_"
    wqkv, bqkv = arr(ffn + "W_qkv"), arr(ffn + "b_qkv")
    lag = np.arange(T)[None, :] - 1 - np.arange(P)[:, None]
    weights = {
        "wq1": by_chunk(arr(attn + "Wq").T), "wk1": by_chunk(arr(attn + "Wk").T), "wv1": by_chunk(arr(attn + "Wv").T),
        "bq1": arr(attn + "bq").reshape(P, 1), "bk1": arr(attn + "bk").reshape(P, 1), "bv1": rows(arr(attn + "bv")),
        "wo1": arr(attn + "Wo").T, "bo1": rows(arr(attn + "bo")),
        "wq2": by_chunk(head_rows(arr(cross + "w_q")).T), "wk2": by_chunk(head_rows(arr(cross + "w_k")).T),
        "wv2": by_chunk(arr(cross + "w_v").T), "wo2": by_chunk(arr(cross + "w_o").T),
        "bq2": head_rows(arr(cross + "b_q")).reshape(DC, P).T, "bk2": head_rows(arr(cross + "b_k")).reshape(DC, P).T,
        "bv2": rows(arr(cross + "b_v")), "bo2": rows(arr(cross + "b_o")),
        "wqkv3": by_chunk(np.concatenate([head_rows(wqkv[:, :D].T).T, head_rows(wqkv[:, D:2 * D].T).T, wqkv[:, 2 * D:]], 1)),
        "bq3": head_rows(bqkv[:D]).reshape(DC, P).T, "bk3": head_rows(bqkv[D:2 * D]).reshape(DC, P).T,
        "bv3": rows(bqkv[2 * D:]),
        "wg": by_chunk(arr(ffn + "W_gate")), "bg": rows(arr(ffn + "b_gate")),
        "we": by_chunk(arr(ffn + "W_experts").transpose(1, 0, 2).reshape(D, E * D)),
        "be": np.concatenate([arr(ffn + "b_experts"), np.zeros((P - E, D), np.float32)], 0),
        "ident": np.eye(P, dtype=np.float32),
        "decay": np.where(lag >= 0, RATE * DECAY ** np.maximum(lag, 0.0), 0.0).astype(np.float32),
        "earlier": rows((np.arange(E)[None, :] < np.arange(E)[:, None]).astype(np.float32)),
    }
    arrays = {"in_x": x, "in_xT": x.transpose(0, 2, 1), "in_ctxT": ctx.transpose(0, 2, 1)}
    arrays.update({"in_" + n: a for n, a in weights.items()})
    arrays = {n: np.ascontiguousarray(a) for n, a in arrays.items()}
    nc = bacc.Bacc("TRN2", target_bir_lowering=False, num_devices=1)
    ap = {n: nc.dram_tensor(n, a.shape, F32, kind="ExternalInput").ap() for n, a in arrays.items()}
    out = nc.dram_tensor("out_0", x.shape, F32, kind="ExternalOutput").ap()
    decoder(nc, ap["in_x"], ap["in_xT"], ap["in_ctxT"], {n: ap["in_" + n] for n in weights}, out)
    r = run(nc, [arrays], core_ids=[0])
    return r.results[0]["out_0"]
```
